# Optimizing a Trainium2 kernel written in Bass

```python
import numpy as np
import jax
import jax.numpy as jnp

def _softmax(x, axis=-1):
    return jax.nn.softmax(x, axis=axis)

def _gelu(x):
    return jax.nn.gelu(x, approximate=True)

def _silu(x):
    return jax.nn.silu(x)

def _sigmoid(x):
    return jax.nn.sigmoid(x)

def _layernorm(x, axis=-1, eps=1e-05):
    m = jnp.mean(x, axis=axis, keepdims=True)
    v = jnp.var(x, axis=axis, keepdims=True)
    return (x - m) / jnp.sqrt(v + eps)

def _scatter_add(tgt, idx, src, axis=0):
    return tgt.at[idx].add(src)

def _segment_sum(src, seg, n):
    return jax.ops.segment_sum(src, seg, n)
kernel_name = 'mk_gnn_resnorm_d4_gnn_r32_f2e241'

def setup_inputs(seed: int=0):
    np.random.seed(seed)
    _w = jnp.asarray

    def _rec_inputs():
        import jax
        import jax.numpy as jnp
        _gk = jax.random.key(seed)
        x = -0.0003713 + 1 * jax.random.normal(jax.random.fold_in(_gk, 1), (3125, 128), jnp.float32)
        src = jax.random.randint(jax.random.fold_in(_gk, 2), (100000,), 0, 3125, jnp.int32)
        dst = jnp.minimum((3125 * jax.random.uniform(jax.random.fold_in(_gk, 3), (100000,)) ** 2.0).astype(jnp.int32), 99999)
        _o = jnp.argsort(dst, stable=True)
        src = src[_o]
        dst = dst[_o]
        return (x, src, dst)
    x, src, dst = _rec_inputs()

    def _L0_gnn_setup():
        import jax, jax.numpy as jnp
        import numpy as np
        N_NODES = 3125
        N_EDGES = 100000
        N_IN = 128
        N_H = 128
        key = jax.random.key(seed)
        k_x, k_e, k_w = jax.random.split(key, 3)
        x = jax.random.normal(k_x, (N_NODES, N_IN), dtype=jnp.float32)
        edge_index = jax.random.randint(k_e, (2, N_EDGES), 0, N_NODES, dtype=jnp.int64)
        W = jax.random.normal(k_w, (N_IN, N_H), dtype=jnp.float32) * (1.0 / np.sqrt(N_IN))
        b = jnp.zeros((N_H,), dtype=jnp.float32)
        a = jnp.float32(0.25)
        return {'x': x, 'edge_index': edge_index, 'W': W, 'b': b, 'a': a}
    _L0_gnn_all = _L0_gnn_setup()
    _L0_gnn_in = {k: v for k, v in _L0_gnn_all.items() if k in ('W', 'b', 'a')}
    del _L0_gnn_all

    def _L1_gnn_setup():
        import jax, jax.numpy as jnp
        import numpy as np
        N_NODES = 3125
        N_EDGES = 50000
        D = 128

        def sage_conv(x, src, dst, W_l, b_l, W_r):
            msgs = x[src]
            agg = jax.ops.segment_sum(msgs, dst, num_segments=x.shape[0])
            deg = jax.ops.segment_sum(jnp.ones((src.shape[0],), x.dtype), dst, num_segments=x.shape[0])
            agg = agg / jnp.maximum(deg, 1.0)[:, None]
            return agg @ W_l.T + b_l + x @ W_r.T
        key = jax.random.key(seed)
        ks = jax.random.split(key, 8)
        s = 1.0 / np.sqrt(D)
        return {'x': jax.random.normal(ks[0], (N_NODES, D), dtype=jnp.float32), 'edge_index': jax.random.randint(ks[1], (2, N_EDGES), 0, N_NODES, dtype=jnp.int64), 'W1_l': jax.random.normal(ks[2], (D, D), dtype=jnp.float32) * s, 'b1': jnp.zeros((D,), dtype=jnp.float32), 'W1_r': jax.random.normal(ks[3], (D, D), dtype=jnp.float32) * s, 'W2_l': jax.random.normal(ks[4], (D, D), dtype=jnp.float32) * s, 'b2': jnp.zeros((D,), dtype=jnp.float32), 'W2_r': jax.random.normal(ks[5], (D, D), dtype=jnp.float32) * s}
    _L1_gnn_all = _L1_gnn_setup()
    _L1_gnn_in = {k: v for k, v in _L1_gnn_all.items() if k in ('W1_l', 'b1', 'W1_r', 'W2_l', 'b2', 'W2_r')}
    del _L1_gnn_all

    def _L2_gnn_setup():
        import jax, jax.numpy as jnp
        import numpy as np
        NUM_LAYERS = 4
        HIDDEN = 128
        N_NODES = 50000
        N_EDGES = 25000

        def _gru_cell(inp, h, w_ih, w_hh, b_ih, b_hh):
            gi = inp @ w_ih.T + b_ih
            gh = h @ w_hh.T + b_hh
            i_r, i_z, i_n = jnp.split(gi, 3, axis=-1)
            h_r, h_z, h_n = jnp.split(gh, 3, axis=-1)
            r = jax.nn.sigmoid(i_r + h_r)
            z = jax.nn.sigmoid(i_z + h_z)
            n = jnp.tanh(i_n + r * h_n)
            return (1.0 - z) * n + z * h
        key = jax.random.key(seed)
        ks = jax.random.split(key, 8)
        s = 1.0 / np.sqrt(HIDDEN)
        node_embed = jax.random.normal(ks[0], (N_NODES, HIDDEN), dtype=jnp.float32)
        edge_index = jax.random.randint(ks[1], (2, N_EDGES), 0, N_NODES, dtype=jnp.int64)
        weight = jax.random.normal(ks[2], (NUM_LAYERS, HIDDEN, HIDDEN), dtype=jnp.float32) * s
        w_ih = jax.random.normal(ks[3], (3 * HIDDEN, HIDDEN), dtype=jnp.float32) * s
        w_hh = jax.random.normal(ks[4], (3 * HIDDEN, HIDDEN), dtype=jnp.float32) * s
        b_ih = jax.random.normal(ks[5], (3 * HIDDEN,), dtype=jnp.float32) * s
        b_hh = jax.random.normal(ks[6], (3 * HIDDEN,), dtype=jnp.float32) * s
        return {'node_embed': node_embed, 'edge_index': edge_index, 'weight': weight, 'w_ih': w_ih, 'w_hh': w_hh, 'b_ih': b_ih, 'b_hh': b_hh}
    _L2_gnn_all = _L2_gnn_setup()
    _L2_gnn_in = {k: v for k, v in _L2_gnn_all.items() if k in ('weight', 'w_ih', 'w_hh', 'b_ih', 'b_hh')}
    del _L2_gnn_all

    def _L3_gnn_setup():
        import jax, jax.numpy as jnp
        import numpy as np
        N = 50000
        E = 25000
        DIN, DH, DOUT, DCTX = (128, 128, 128, 64)

        def gcn_conv(x, src, dst, W, b):
            n = x.shape[0]
            h = x @ W
            loop = jnp.arange(n, dtype=src.dtype)
            s = jnp.concatenate([src, loop])
            d = jnp.concatenate([dst, loop])
            deg = jax.ops.segment_sum(jnp.ones(s.shape, h.dtype), d, num_segments=n)
            dinv = jax.lax.rsqrt(jnp.maximum(deg, 1.0))
            norm = dinv[s] * dinv[d]
            msgs = h[s] * norm[:, None]
            return jax.ops.segment_sum(msgs, d, num_segments=n) + b
        key = jax.random.key(seed)
        ks = jax.random.split(key, 8)
        x = jax.random.normal(ks[0], (N, DIN), jnp.float32)
        edge_index = jax.random.randint(ks[1], (2, E), 0, N, dtype=jnp.int64)
        ctx = jax.random.normal(ks[2], (1, DCTX), jnp.float32)
        init = lambda k, shp, fan: jax.random.normal(k, shp, jnp.float32) / np.sqrt(fan).astype(np.float32)
        W1 = init(ks[3], (DIN, DH), DIN)
        b1 = jnp.zeros((DH,), jnp.float32)
        W2 = init(ks[4], (DH, DOUT), DH)
        b2 = jnp.zeros((DOUT,), jnp.float32)
        Wg = init(ks[5], (DCTX, DOUT), DCTX)
        bg = jnp.zeros((DOUT,), jnp.float32)
        Wb = init(ks[6], (DCTX, DOUT), DCTX)
        return {'x': x, 'ctx': ctx, 'W1': W1, 'b1': b1, 'W2': W2, 'b2': b2, 'Wg': Wg, 'bg': bg, 'Wb': Wb, 'edge_index': edge_index}
    _L3_gnn_all = _L3_gnn_setup()
    _L3_gnn_in = {k: v for k, v in _L3_gnn_all.items() if k in ('ctx', 'W1', 'b1', 'W2', 'b2', 'Wg', 'bg', 'Wb')}
    del _L3_gnn_all
    return {'x': x, 'src': src, 'dst': dst, 'L0_gnn_W': _L0_gnn_in['W'], 'L0_gnn_b': _L0_gnn_in['b'], 'L0_gnn_a': _L0_gnn_in['a'], 'L1_gnn_W1_l': _L1_gnn_in['W1_l'], 'L1_gnn_b1': _L1_gnn_in['b1'], 'L1_gnn_W1_r': _L1_gnn_in['W1_r'], 'L1_gnn_W2_l': _L1_gnn_in['W2_l'], 'L1_gnn_b2': _L1_gnn_in['b2'], 'L1_gnn_W2_r': _L1_gnn_in['W2_r'], 'L2_gnn_weight': _L2_gnn_in['weight'], 'L2_gnn_w_ih': _L2_gnn_in['w_ih'], 'L2_gnn_w_hh': _L2_gnn_in['w_hh'], 'L2_gnn_b_ih': _L2_gnn_in['b_ih'], 'L2_gnn_b_hh': _L2_gnn_in['b_hh'], 'L3_gnn_ctx': _L3_gnn_in['ctx'], 'L3_gnn_W1': _L3_gnn_in['W1'], 'L3_gnn_b1': _L3_gnn_in['b1'], 'L3_gnn_W2': _L3_gnn_in['W2'], 'L3_gnn_b2': _L3_gnn_in['b2'], 'L3_gnn_Wg': _L3_gnn_in['Wg'], 'L3_gnn_bg': _L3_gnn_in['bg'], 'L3_gnn_Wb': _L3_gnn_in['Wb']}

def reference(x, src, dst, L0_gnn_W, L0_gnn_b, L0_gnn_a, L1_gnn_W1_l, L1_gnn_b1, L1_gnn_W1_r, L1_gnn_W2_l, L1_gnn_b2, L1_gnn_W2_r, L2_gnn_weight, L2_gnn_w_ih, L2_gnn_w_hh, L2_gnn_b_ih, L2_gnn_b_hh, L3_gnn_ctx, L3_gnn_W1, L3_gnn_b1, L3_gnn_W2, L3_gnn_b2, L3_gnn_Wg, L3_gnn_bg, L3_gnn_Wb):
    import jax
    import jax.numpy as jnp

    def _L0_gnn_ref(x, edge_index, W, b, a):
        import jax, jax.numpy as jnp
        import numpy as np
        N_NODES = 3125
        N_EDGES = 100000
        N_IN = 128
        N_H = 128
        n = x.shape[0]
        src, dst = (edge_index[0], edge_index[1])
        loop = jnp.arange(n, dtype=src.dtype)
        src_l = jnp.concatenate([src, loop])
        dst_l = jnp.concatenate([dst, loop])
        deg = jax.ops.segment_sum(jnp.ones_like(src_l, dtype=x.dtype), dst_l, num_segments=n)
        dinv = deg ** (-0.5)
        norm = dinv[src_l] * dinv[dst_l]
        h = x @ W
        msg = h[src_l] * norm[:, None]
        agg = jax.ops.segment_sum(msg, dst_l, num_segments=n)
        out = agg + b
        return jnp.where(out > 0, out, a * out)

    def _L1_gnn_ref(x, edge_index, W1_l, b1, W1_r, W2_l, b2, W2_r):
        import jax, jax.numpy as jnp
        import numpy as np
        N_NODES = 3125
        N_EDGES = 50000
        D = 128

        def sage_conv(x, src, dst, W_l, b_l, W_r):
            msgs = x[src]
            agg = jax.ops.segment_sum(msgs, dst, num_segments=x.shape[0])
            deg = jax.ops.segment_sum(jnp.ones((src.shape[0],), x.dtype), dst, num_segments=x.shape[0])
            agg = agg / jnp.maximum(deg, 1.0)[:, None]
            return agg @ W_l.T + b_l + x @ W_r.T
        src, dst = (edge_index[0], edge_index[1])
        h = jax.nn.relu(sage_conv(x, src, dst, W1_l, b1, W1_r))
        out = sage_conv(h, src, dst, W2_l, b2, W2_r)
        return out

    def _L2_gnn_ref(node_embed, edge_index, weight, w_ih, w_hh, b_ih, b_hh):
        import jax, jax.numpy as jnp
        import numpy as np
        NUM_LAYERS = 4
        HIDDEN = 128
        N_NODES = 50000
        N_EDGES = 25000

        def _gru_cell(inp, h, w_ih, w_hh, b_ih, b_hh):
            gi = inp @ w_ih.T + b_ih
            gh = h @ w_hh.T + b_hh
            i_r, i_z, i_n = jnp.split(gi, 3, axis=-1)
            h_r, h_z, h_n = jnp.split(gh, 3, axis=-1)
            r = jax.nn.sigmoid(i_r + h_r)
            z = jax.nn.sigmoid(i_z + h_z)
            n = jnp.tanh(i_n + r * h_n)
            return (1.0 - z) * n + z * h
        src = edge_index[0]
        dst = edge_index[1]
        n_nodes = node_embed.shape[0]
        x = node_embed
        for l in range(NUM_LAYERS):
            m = x @ weight[l]
            agg = jax.ops.segment_sum(m[src], dst, num_segments=n_nodes)
            x = _gru_cell(agg, x, w_ih, w_hh, b_ih, b_hh)
        return x + node_embed

    def _L3_gnn_ref(x, ctx, W1, b1, W2, b2, Wg, bg, Wb, edge_index):
        import jax, jax.numpy as jnp
        import numpy as np
        N = 50000
        E = 25000
        DIN, DH, DOUT, DCTX = (128, 128, 128, 64)

        def gcn_conv(x, src, dst, W, b):
            n = x.shape[0]
            h = x @ W
            loop = jnp.arange(n, dtype=src.dtype)
            s = jnp.concatenate([src, loop])
            d = jnp.concatenate([dst, loop])
            deg = jax.ops.segment_sum(jnp.ones(s.shape, h.dtype), d, num_segments=n)
            dinv = jax.lax.rsqrt(jnp.maximum(deg, 1.0))
            norm = dinv[s] * dinv[d]
            msgs = h[s] * norm[:, None]
            return jax.ops.segment_sum(msgs, d, num_segments=n) + b
        src, dst = (edge_index[0], edge_index[1])
        gate = jax.nn.sigmoid(ctx @ Wg + bg)
        bias = ctx @ Wb
        h = jax.nn.leaky_relu(gcn_conv(x, src, dst, W1, b1), negative_slope=0.2)
        out = gcn_conv(h, src, dst, W2, b2)
        return out * gate + bias
    edge_index = jnp.stack([src, dst])
    x = _layernorm(x + _L0_gnn_ref(x, edge_index, L0_gnn_W, L0_gnn_b, L0_gnn_a), axis=-1)
    x = _layernorm(x + _L1_gnn_ref(x, edge_index, L1_gnn_W1_l, L1_gnn_b1, L1_gnn_W1_r, L1_gnn_W2_l, L1_gnn_b2, L1_gnn_W2_r), axis=-1)
    x = _layernorm(x + _L2_gnn_ref(x, edge_index, L2_gnn_weight, L2_gnn_w_ih, L2_gnn_w_hh, L2_gnn_b_ih, L2_gnn_b_hh), axis=-1)
    x = _layernorm(x + _L3_gnn_ref(x, L3_gnn_ctx, L3_gnn_W1, L3_gnn_b1, L3_gnn_W2, L3_gnn_b2, L3_gnn_Wg, L3_gnn_bg, L3_gnn_Wb, edge_index), axis=-1)
    return x

_drawn_inputs = setup_inputs


def setup_inputs(seed=0):
    import zlib

    import numpy as np

    out = dict(_drawn_inputs(seed))
    spreads = {'L0_gnn_b': (0.0, 0.1),
     'L1_gnn_b1': (0.0, 0.1),
     'L1_gnn_b2': (0.0, 0.1),
     'L3_gnn_b1': (0.0, 0.294),
     'L3_gnn_b2': (0.0, 0.1),
     'L3_gnn_bg': (0.0, 0.8)}
    factors = {}
    for name, (base, spread) in spreads.items():
        noise = np.random.default_rng([zlib.crc32(name.encode()), seed]).standard_normal(out[name].shape)
        drawn = base * np.exp(spread * noise) if base else spread * noise
        out[name] = jnp.asarray(drawn.astype(out[name].dtype))
    for name, factor in factors.items():
        out[name] = (out[name] * factor).astype(out[name].dtype)
    return out
```

```python
from contextlib import ExitStack

import concourse.bass as bass
from concourse import mybir

F32 = mybir.dt.float32
F16 = mybir.dt.float16
BF16 = mybir.dt.bfloat16
I32 = mybir.dt.int32
ALU = mybir.AluOpType
ACT = mybir.ActivationFunctionType
AX = mybir.AxisListType

D = 128
P = 125
N = 3125
NC = N // P
E = 100000
EC = E // P
W = 20
WC = NC * W
NWIN = -(-N // W)
LASTW = N - (NWIN - 1) * W
K = 4
RING = 2
ECP = EC + K
WP = (NWIN + 1) // 2
EP, EJ = 100, 8
BIG = 1024.0
HALF = 0.5
ROUND = 12582912.0
CPB = 4
NB = -(-NC // CPB)
SCALE = 4096.0
ROWB = 11.5
EPS = 1e-5


def chunks_of(b):
    return min(CPB, NC - CPB * b)


def build(nc, x_d, src_d, dst_d, w0_d, b0_d, a_d, w1l_d, b1_d, w1r_d, w2l_d, b2_d, w2r_d,
          gw_d, wih_d, whh_d, bih_d, bhh_d, ctx_d, w31_d, b31_d, w32_d, b32_d, wg_d, bg_d, wb_d, out_d):
    cm_s = nc.dram_tensor("chunk_bounds", [2, EC], F32, kind="Internal").ap()
    tab_s = nc.dram_tensor("window_table", [WP * 8], I32, kind="Internal").ap()
    wt_s = nc.dram_tensor("weights_turned", [4, D, D], F32, kind="Internal").ap()
    whh_s = nc.dram_tensor("whh_turned", [D, 3 * D], F32, kind="Internal").ap()
    wc_s = nc.dram_tensor("gate_weights", [4, D, 3 * D], F32, kind="Internal").ap()
    rows_s = nc.dram_tensor("gate_rows", [2, D], F32, kind="Internal").ap()
    x2_s = nc.dram_tensor("x2", [N, D], F32, kind="Internal").ap()

    with ExitStack() as ctx:
        def sem(name):
            return ctx.enter_context(nc.semaphore(name))

        ATX = ctx.enter_context(nc.sbuf_tensor("counts", [P + 1, NC, N], F16))
        AT = ATX[0:P]
        ARENA = 56576
        arena = ctx.enter_context(nc.sbuf_tensor("arena", [128, ARENA // 4], F32))

        def at(off, count, dt=F32, parts=128):
            size = 2 if dt in (F16, BF16) else 4
            assert off % 4 == 0 and off + count * size <= ARENA, (off, count)
            words = -(-count * size // 4)
            v = arena[0:parts, off // 4:off // 4 + words]
            return (v if dt == F32 else v.bitcast(dt))[:, 0:count]

        O_XT, O_PA, O_PB, O_AG = 0, 12512, 31712, 44512
        O_XS, O_U, O_W = 46528, 48576, 50624
        O_ID, O_SM = 54208, 54720
        XT = at(O_XT, N)
        PA = [at(O_PA + 6400 * k, NC * D, F16, P).rearrange("p (c f) -> p c f", f=D) for k in range(2)]
        PB = [at(O_PB + 6400 * k, NC * D, F16, P).rearrange("p (c f) -> p c f", f=D) for k in range(2)]
        AG = at(O_AG, CPB * P)
        XS = at(O_XS, CPB * P)
        RX = at(O_XS, CPB * D, F32, P).rearrange("p (c f) -> p c f", f=D)
        U2 = [at(o, CPB * D, F32, P).rearrange("p (c f) -> p c f", f=D) for o in (O_U, O_PA + 12800)]
        XALL = at(O_PB, NC * D, F32, P).rearrange("p (c f) -> p c f", f=D)
        WA = at(O_W, D)
        WB = at(O_W + 512, D)
        BB = at(O_W + 1024, D, F32, P)
        T = at(O_W + 1536, CPB * D, F32, P).rearrange("p (c f) -> p c f", f=D)
        WCG = at(O_W, 3 * D)
        WHH = at(O_W + 1536, 3 * D)
        O_P3 = O_PA + 12800
        GR = at(O_XS, CPB * P)
        GZ = at(O_U, CPB * P)
        GT = at(O_P3, CPB * P)
        NX = at(O_P3 + 2000, CPB * P)
        Y = at(O_P3 + 4000, CPB * D, F32, P).rearrange("p (c f) -> p c f", f=D)
        ident = at(O_ID, D)
        o = O_SM
        small = {}
        for name, cnt in (("dinv", NC), ("s1", NC), ("sd", NC), ("mv", 2 * CPB), ("rs", CPB), ("ab", 1),
                          ("gb", 6), ("st", 6 * CPB), ("sq", 3), ("mx", 3), ("sc", 3), ("si", 3), ("bd", 3), ("bc", 2)):
            small[name] = at(o, cnt)
            o += cnt * 4
        dinv, s1, sd = (small[k][0:P] for k in ("dinv", "s1", "sd"))
        mv = small["mv"][0:P].rearrange("p (c t) -> p c t", t=2)
        st = small["st"][0:P].rearrange("p (c t) -> p c t", t=6)
        rs, ab = small["rs"][0:P], small["ab"][0:P]
        gb = small["gb"]
        sq, mx, sc, si, bd, bc = (small[k] for k in ("sq", "mx", "sc", "si", "bd", "bc"))
        ones = at(o, 2, F16, P)
        W31R = at(42496, D)
        SQT = at(43520, D)
        XE = at(10880, NC * D, F32, P)
        DEGR = at(0, N, F16, NC)

        iotax = at(0, WC * K, F16, P).rearrange("p (n k) -> p n k", k=K)
        KEY = at(4000, ECP, F32, P)
        LO = at(7216, ECP, F16, P)
        LR = at(8832, RING * K * 128, F16, P)
        MR = at(10880, RING * K * WC, F16, P)
        KR = at(26880, RING * K, F16, P)
        WT = at(26896, NWIN, F32, P)
        ZZ = at(27524, 128, F16, P)
        TAB = at(27780, WP * 8, I32, 1)
        ei = at(10880, EJ * P, I32, EP)
        ef = at(14880, EJ * P, F32, EP)
        eh = at(18880, EJ * P, F32, EP)
        es = at(22880, EJ * P, F32, EP)
        di = at(30400, EJ * P, I32, EP)
        df = at(34400, EJ * P, F32, EP)
        dw = at(38400, EJ * P, F32, EP)
        CM = at(42400, 2 * EJ, F32, EP)
        CB = at(30400, 2 * EC, F32, WP)
        CI = at(36800, EC, F32, WP)
        TMP = at(40000, EC, F32, WP)
        WID = at(43200, 2, F32, WP)
        WM = at(43208, 8, F32, WP)
        TBI = at(43240, 8, I32, WP)
        WR = at(O_AG, 14 * D)
        TW = at(0, 14 * D)
        WCT = at(10880, 12 * D)
        row = at(51680, 4 * D, F32, 1)
        ctxc = at(53728, 1, F32, 64)
        WGB = at(7216, 2 * D, F32, 64)

        ps = [ctx.enter_context(nc.psum_tensor(f"bank{i}", [128, 512], F32)) for i in range(8)]

        names = ("x_in x_early sums_ready max_ready deg_in sums_done max_done bounds_root scales_ready weights_in edges_in sources_in consts weights_turned turned_kept wc_mm wc_done wc_kept rows_mm gate_pre "
                 "gate_done rows_done rows_kept dve_step keys_turned keys_kept cm_stored cm_back tab_stored "
                 "tab_back pool_step key_rel hot_ready hot_free win_done win_kept deg_mm deg_plus deg_root stage_w rx_in "
                 "rx_free parts_done agg_done ag_ready dense_done dense_free xs_ready xt_ready u_ready tn_done "
                 "tn_free tf_done sd_ready var_ready r_ready z_ready pre_n n_ready nx_ready nx_copied x2_stored0 "
                 "x2_stored1 out_stored0 out_stored1").split()
        S = {n: sem(n) for n in names}
        block = ctx.enter_context(nc.Block())

        STAGES = [("prep", None, PA), ("gcn0", PA, PB), ("sage1", PB, PA), ("sage2", PA, PB),
                  ("gru", PB, PA), ("gru", PA, PB), ("gru", PB, PA),
                  ("gru_last", PA, PB), ("gcn1", PB, PA), ("gcn2", PA, None)]
        NS = len(STAGES)
        gru_no = {4: 0, 5: 1, 6: 2, 7: 3}

        def cols(b):
            return P * b * CPB, P * chunks_of(b)

        plan = {}
        total = {}

        def event(name, key, inc=1):
            total[name] = total.get(name, 0) + inc
            plan[(name,) + key] = total[name]

        for s, (kind, pin, pout) in enumerate(STAGES):
            if kind != "prep":
                event("stage_w", (s,), 16 * {"gcn0": 2, "sage1": 3, "sage2": 3, "gru": 2, "gru_last": 2, "gcn1": 2, "gcn2": 3}[kind])
            for b in range(NB):
                k = (s, b)
                own = []
                if kind in ("gcn0", "gru_last"):
                    event("rx_in", k, 16)
                if kind == "gcn0":
                    own += ["rx_free"]
                if kind != "prep":
                    own += ["agg_done", "ag_ready", "dense_done"]
                if kind in ("gcn0", "sage1", "sage2", "gcn1", "gcn2"):
                    own += ["dense_free", "u_ready"]
                if kind in ("prep", "gru_last"):
                    own += ["u_ready"]
                if kind.startswith("sage"):
                    own += ["xs_ready"]
                if kind not in ("gru", "gcn2"):
                    own += ["tf_done", "xt_ready"]
                if kind.startswith("gru"):
                    own += ["r_ready", "z_ready", "pre_n", "n_ready", "nx_ready", "tn_done"]
                if kind == "gru":
                    own += ["nx_copied"]
                if kind == "gru_last":
                    own += ["tn_free"]
                if kind in ("gcn0", "sage2", "gru_last", "gcn2"):
                    own += ["var_ready", "sd_ready"]
                if pout is not None:
                    own += ["parts_done"]
                for n in own:
                    event(n, k)
                if kind == "sage2":
                    event(f"x2_stored{b % 2}", k, 16)
                if kind == "gcn2":
                    event(f"out_stored{b % 2}", k, 16)

        def val(name, s, b=None):
            return plan[(name, s) if b is None else (name, s, b)]

        def before(name, s, b):
            keys = [(name, t, c) for t in range(s + 1) for c in range(NB) if (t, c) < (s, b)]
            for k in reversed(keys):
                if k in plan:
                    return plan[k]
            return None

        step_at = {"bounds": 7, "keyd": 15, "table": 37}

        @block.sync
        def _(sp):
            for k, w in enumerate((w1l_d, w1r_d, w2l_d, w2r_d)):
                sp.dma_start(WR[:, k * D:(k + 1) * D], w).then_inc(S["weights_in"], 16)
            sp.dma_start(WR[:, 4 * D:7 * D].rearrange("p (g i) -> p g i", g=3),
                         wih_d.rearrange("(g p) i -> p g i", p=D)).then_inc(S["weights_in"], 16)
            sp.dma_start(WR[:, 7 * D:10 * D].rearrange("p (g i) -> p g i", g=3),
                         whh_d.rearrange("(g p) i -> p g i", p=D)).then_inc(S["weights_in"], 16)
            sp.dma_start(WR[:, 10 * D:14 * D].rearrange("p (l i) -> p l i", l=4),
                         gw_d.rearrange("l p i -> p l i")).then_inc(S["weights_in"], 16)
            sp.dma_start(WGB[:, 0:D], wg_d).then_inc(S["weights_in"], 16)
            sp.dma_start(WGB[:, D:2 * D], wb_d).then_inc(S["weights_in"], 16)
            sp.dma_start(ctxc, ctx_d.rearrange("a k -> k a")).then_inc(S["weights_in"], 16)
            sp.dma_start(W31R, w31_d).then_inc(S["weights_in"], 16)
            sp.dma_start(bc[:, 0:1], b1_d.rearrange("(p a) -> p a", a=1)).then_inc(S["weights_in"], 16)
            sp.dma_start(bc[:, 1:2], b31_d.rearrange("(p a) -> p a", a=1)).then_inc(S["weights_in"], 16)
            sp.dma_start(row[:, 0:D], bg_d.rearrange("(a k) -> a k", a=1)).then_inc(S["weights_in"], 16)
            sp.dma_start(row[:, D:2 * D], b32_d.rearrange("(a k) -> a k", a=1)).then_inc(S["weights_in"], 16)
            sp.dma_start(di, dst_d.rearrange("(p f) -> p f", p=EP)).then_inc(S["edges_in"], 16)
            sp.dma_start(gb[:, 0:3], bih_d.rearrange("(g p) -> p g", p=D), allow_slow_non_contiguous=True).then_inc(S["weights_in"], 16)
            sp.dma_start(gb[:, 3:6], bhh_d.rearrange("(g p) -> p g", p=D), allow_slow_non_contiguous=True).then_inc(S["weights_in"], 16)
            sp.dma_start(ab, a_d.rearrange("(a b) -> a b", a=1).to_broadcast([P, 1])).then_inc(S["weights_in"], 16)
            sp.wait_ge(S["turned_kept"], 4)
            sp.dma_start(wt_s.rearrange("k p i -> p k i"),
                         TW[:, 0:4 * D].rearrange("p (k i) -> p k i", k=4)).then_inc(S["wc_kept"], 16)
            sp.dma_start(whh_s, TW[:, 7 * D:10 * D]).then_inc(S["wc_kept"], 16)
            sp.wait_ge(S["wc_done"], 4)
            sp.dma_start(wc_s.rearrange("l p i -> p l i"),
                         WCT.rearrange("p (l i) -> p l i", l=4)).then_inc(S["wc_kept"], 16)
            sp.wait_ge(S["wc_kept"], 48)
            sp.dma_start(ei, src_d.rearrange("(p f) -> p f", p=EP)).then_inc(S["sources_in"], 16)
            sp.wait_ge(S["rows_done"], 1)
            sp.dma_start(rows_s, row[:, 2 * D:4 * D]).then_inc(S["rows_kept"], 16)
            sp.wait_ge(S["dve_step"], step_at["bounds"])
            sp.dma_start(cm_s.rearrange("t (p j) -> p t j", p=EP),
                         CM.rearrange("p (t j) -> p t j", t=2)).then_inc(S["cm_stored"], 16)
            sp.wait_ge(S["cm_stored"], 16)
            sp.wait_ge(S["keys_kept"], 4)
            sp.dma_start(XE.rearrange("p (c f) -> p c f", f=D), x_d.rearrange("(c p) f -> p c f", p=P)).then_inc(S["x_early"], 16)
            for t in range(2):
                sp.dma_start(CB[:, t * EC:(t + 1) * EC], cm_s[t:t + 1, :].to_broadcast([WP, EC])).then_inc(S["cm_back"], 16)
            sp.wait_ge(S["dve_step"], step_at["table"])
            sp.dma_start(tab_s.rearrange("(p k) -> p k", p=WP), TBI).then_inc(S["tab_stored"], 16)
            sp.wait_ge(S["tab_stored"], 16)
            sp.dma_start(TAB, tab_s.rearrange("(a k) -> a k", a=1)).then_inc(S["tab_back"], 16)
            sp.dma_start(XALL, x_d.rearrange("(c p) f -> p c f", p=P)).then_inc(S["x_in"], 16)
            sp.wait_ge(S["rows_kept"], 16)
            sp.wait_ge(S["win_kept"], 2 + NWIN)
            sp.dma_start(DEGR, ATX[P:P + 1].rearrange("p c d -> p (c d)")).then_inc(S["deg_in"], 16)

            xv = x_d.rearrange("(c p) f -> p c f", p=P)
            x2v = x2_s.rearrange("(c p) f -> p c f", p=P)
            ov = out_d.rearrange("(c p) f -> p c f", p=P)
            for s, (kind, pin, pout) in enumerate(STAGES):
                if kind != "prep":
                    v = before("dense_done", s, 0)
                    if v:
                        sp.wait_ge(S["dense_done"], v)
                    v = before("parts_done", s, 0)
                    if v:
                        sp.wait_ge(S["parts_done"], v)
                q = S["stage_w"]
                if kind == "gcn0":
                    sp.dma_start(WA, w0_d).then_inc(q, 16)
                    sp.dma_start(BB, b0_d.rearrange("(a k) -> a k", a=1).to_broadcast([P, D])).then_inc(q, 16)
                if kind in ("sage1", "sage2"):
                    k = 0 if kind == "sage1" else 2
                    sp.dma_start(WA, wt_s[k]).then_inc(q, 16)
                    sp.dma_start(WB, wt_s[k + 1]).then_inc(q, 16)
                    bias = b1_d if kind == "sage1" else b2_d
                    sp.dma_start(BB, bias.rearrange("(a k) -> a k", a=1).to_broadcast([P, D])).then_inc(q, 16)
                if kind.startswith("gru"):
                    sp.dma_start(WCG, wc_s[gru_no[s]]).then_inc(q, 16)
                    sp.dma_start(WHH, whh_s).then_inc(q, 16)
                if kind == "gcn1":
                    sp.dma_start(WA, w31_d).then_inc(q, 16)
                    sp.dma_start(BB, b31_d.rearrange("(a k) -> a k", a=1).to_broadcast([P, D])).then_inc(q, 16)
                if kind == "gcn2":
                    sp.dma_start(WA, w32_d).then_inc(q, 16)
                    sp.dma_start(WB[0:P], rows_s[0:1, :].to_broadcast([P, D])).then_inc(q, 16)
                    sp.dma_start(BB, rows_s[1:2, :].to_broadcast([P, D])).then_inc(q, 16)
                for b in range(NB):
                    n = chunks_of(b)
                    cs = slice(CPB * b, CPB * b + n)
                    if kind in ("gcn0", "gru_last"):
                        if kind == "gcn0" and b:
                            sp.wait_ge(S["rx_free"], val("rx_free", s, b - 1))
                        if kind == "gru_last" and b:
                            sp.wait_ge(S["parts_done"], val("parts_done", s, b - 1))
                            sp.wait_ge(S["tf_done"], val("tf_done", s, b - 1))
                        if kind == "gru_last" and b == 0:
                            for i in ("x2_stored0", "x2_stored1"):
                                sp.wait_ge(S[i], total[i])
                        to = Y if kind == "gru_last" else RX
                        frm = x2v if kind == "gru_last" else xv
                        sp.dma_start(to[:, 0:n, :], frm[:, cs, :]).then_inc(S["rx_in"], 16)
                    if kind == "sage2":
                        sp.wait_ge(S["u_ready"], val("u_ready", s, b))
                        sp.dma_start(x2v[:, cs, :], U2[b % 2][:, 0:n, :]).then_inc(S[f"x2_stored{b % 2}"], 16)
                    if kind == "gcn2":
                        sp.wait_ge(S["u_ready"], val("u_ready", s, b))
                        sp.dma_start(ov[:, cs, :], U2[b % 2][:, 0:n, :]).then_inc(S[f"out_stored{b % 2}"], 16)
            for i in ("out_stored0", "out_stored1"):
                sp.wait_ge(S[i], total[i])

        @block.gpsimd
        def _(pool):
            pool.memset(ident, 0.0).then_inc(S["consts"], 1)
            pool.wait_ge(S["consts"], 1)
            pool.affine_select(out=ident, in_=ident, compare_op=ALU.not_equal, fill=1.0, base=0,
                               pattern=[[-1, D]], channel_multiplier=1).then_inc(S["consts"], 1)
            pool.iota(WT, [[W * NC, NWIN]], base=0, channel_multiplier=0,
                      allow_small_or_imprecise_dtypes=True).then_inc(S["consts"], 1)
            pool.memset(ZZ, 0.0).then_inc(S["consts"], 1)
            pool.memset(ones, 1.0).then_inc(S["consts"], 1)
            lrv = LR.rearrange("p (r k b) -> p r k b", r=RING, b=K)
            pool.memset(lrv[:, :, P:P + 1, :], 1.0).then_inc(S["consts"], 1)
            pool.memset(lrv[:, :, P + 1:128, :], 0.0).then_inc(S["consts"], 1)
            pool.wait_ge(S["wc_kept"], 48)
            pool.iota(iotax, [[1, WC], [0, K]], base=0, channel_multiplier=0,
                      allow_small_or_imprecise_dtypes=True).then_inc(S["consts"], 1)
            pool.memset(KEY[:, EC:ECP], -1.0).then_inc(S["consts"], 1)
            pool.wait_ge(S["rows_mm"], 1)
            pool.memset(LO[:, EC:ECP], -1.0).then_inc(S["consts"], 1)
            pool.wait_ge(S["keys_turned"], 4)
            pool.wait_ge(S["dve_step"], step_at["bounds"])
            pool.iota(CI, [[1, EC]], base=0, channel_multiplier=0,
                      allow_small_or_imprecise_dtypes=True).then_inc(S["consts"], 1)
            pool.iota(WID, [[1, 2]], base=0, channel_multiplier=2,
                      allow_small_or_imprecise_dtypes=True).then_inc(S["consts"], 1)
            pool.wait_ge(S["sums_ready"], 1)
            pool.partition_all_reduce(sq, sq, 128, bass.bass_isa.ReduceOp.add).then_inc(S["sums_done"], 1)
            pool.wait_ge(S["max_ready"], 1)
            pool.partition_all_reduce(mx, mx, 128, bass.bass_isa.ReduceOp.max).then_inc(S["max_done"], 1)

        CONST_EARLY, CONST_IOTAX, CONST_ALL = 7, 8, 12

        @block.vector
        def _(dve):
            n = [0]
            made = {}

            def step(ins, name=None):
                if name is None:
                    n[0] += 1
                    ins.then_inc(S["dve_step"], 1)
                    dve.wait_ge(S["dve_step"], n[0])
                else:
                    made[name] = made.get(name, 0) + 1
                    ins.then_inc(S[name], 1)
                    dve.wait_ge(S[name], made[name])

            dve.wait_ge(S["edges_in"], 16)
            step(dve.tensor_copy(df, di))
            step(dve.tensor_scalar(dw, df, 1.0 / W, -0.5 + 0.5 / W, ALU.mult, ALU.add))
            step(dve.tensor_scalar(dw, dw, ROUND, None, ALU.add))
            step(dve.tensor_scalar(dw, dw, ROUND, None, ALU.subtract))
            dwv = dw.rearrange("p (j i) -> p j i", j=EJ)
            dve.tensor_reduce(CM[:, 0:EJ], dwv, AX.X, ALU.max)
            step(dve.tensor_reduce(CM[:, EJ:2 * EJ], dwv, AX.X, ALU.min))
            step(dve.scalar_tensor_tensor(df, dw, float(WC - W), df, ALU.mult, ALU.add))
            step(dve.tensor_copy(dw, df))
            assert n[0] == step_at["bounds"]
            dve.wait_ge(S["rows_mm"], 1)
            dve.tensor_tensor(row[:, 2 * D:3 * D], ps[7][0:1, 0:D], row[:, 0:D], ALU.add).then_inc(S["gate_pre"], 1)
            dve.tensor_tensor(gb[:, 0:2], gb[:, 0:2], gb[:, 3:5], ALU.add)
            dve.wait_ge(S["weights_in"], 16 * 18)
            for j, w in enumerate((WR[:, 0:D], WR[:, D:2 * D], W31R)):
                step(dve.tensor_tensor_reduce(SQT, w, w, 1.0, 0.0, ALU.mult, ALU.add, sq[:, j:j + 1]),
                     None if j < 2 else "sums_ready")
            dve.scalar_tensor_tensor(mx[:, 0:2], bc, -1.0, bc, ALU.mult, ALU.max)
            dve.memset(mx[:, 2:3], 0.0)
            dve.wait_ge(S["sources_in"], 16)
            step(dve.tensor_copy(ef, ei))
            step(dve.tensor_scalar(eh, ef, 1.0 / P, -0.5 + 0.5 / P, ALU.mult, ALU.add))
            step(dve.tensor_scalar(eh, eh, ROUND, None, ALU.add))
            step(dve.tensor_scalar(eh, eh, ROUND, None, ALU.subtract))
            step(dve.scalar_tensor_tensor(es, eh, -float(P), ef, ALU.mult, ALU.add))
            step(dve.scalar_tensor_tensor(dw, eh, float(W), dw, ALU.mult, ALU.add))
            assert n[0] == step_at["keyd"]
            dve.wait_ge(S["gate_done"], 1)
            step(dve.tensor_tensor(row[:, 3 * D:4 * D], row[:, 2 * D:3 * D], row[:, D:2 * D], ALU.mult))
            dve.tensor_tensor(row[:, 3 * D:4 * D], row[:, 3 * D:4 * D], ps[7][0:1, D:2 * D],
                              ALU.add).then_inc(S["rows_done"], 1)
            for g in range(4):
                dve.wait_ge(S["keys_turned"], g + 1)
                what = KEY if g < 2 else LO
                to = what[:, 0:EC].rearrange("p (c j) -> p j c", j=EJ)[:, 4 * (g % 2):4 * (g % 2) + 4, :]
                if g == 2:
                    dve.wait_ge(S["rows_mm"], 1)
                if g == 0:
                    dve.wait_ge(S["wc_kept"], 48)
                dve.tensor_scalar(to, ps[6][0:P, 0:4 * EP].rearrange("p (j c) -> p j c", j=4),
                                  1.0 if g < 2 else HALF, None, ALU.mult).then_inc(S["keys_kept"], 1)
            dve.wait_ge(S["consts"], CONST_IOTAX)
            step(dve.tensor_scalar(iotax, iotax, HALF, None, ALU.mult))
            dve.wait_ge(S["cm_back"], 32)
            dve.wait_ge(S["consts"], CONST_ALL)
            for q in range(2):
                step(dve.tensor_scalar(TMP, CI, -1.0, BIG, ALU.mult, ALU.add))
                step(dve.scalar_tensor_tensor(TMP, CB[:, 0:EC], WID[:, q:q + 1], TMP, ALU.is_ge, ALU.mult))
                step(dve.tensor_reduce(WM[:, q:q + 1], TMP, AX.X, ALU.max))
                step(dve.tensor_scalar(TMP, CI, 1.0, None, ALU.add))
                step(dve.scalar_tensor_tensor(TMP, CB[:, EC:2 * EC], WID[:, q:q + 1], TMP, ALU.is_le, ALU.mult))
                step(dve.tensor_reduce(WM[:, 2 + q:3 + q], TMP, AX.X, ALU.max))
            step(dve.tensor_scalar(WM[:, 0:2], WM[:, 0:2], -1.0, BIG, ALU.mult, ALU.add))
            step(dve.tensor_scalar(WM[:, 0:2], WM[:, 0:2], float(EC - 1), None, ALU.min))
            step(dve.tensor_tensor(WM[:, 4:6], WM[:, 2:4], WM[:, 0:2], ALU.subtract))
            step(dve.tensor_scalar(WM[:, 4:6], WM[:, 4:6], 1.0 / K, 0.5 - 0.5 / K, ALU.mult, ALU.add))
            tb = TBI.rearrange("p (q k) -> p q k", q=2)
            step(dve.tensor_scalar(WM[:, 4:6], WM[:, 4:6], ROUND, None, ALU.add))
            step(dve.tensor_scalar(WM[:, 4:6], WM[:, 4:6], ROUND, None, ALU.subtract))
            dve.tensor_scalar(WM[:, 4:6], WM[:, 4:6], 1.0, None, ALU.max)
            step(dve.memset(TBI, 0))
            dve.tensor_copy(tb[:, :, 0:1], WM[:, 0:2].rearrange("p (q k) -> p q k", k=1))
            step(dve.tensor_copy(tb[:, :, 1:2], WM[:, 4:6].rearrange("p (q k) -> p q k", k=1)))
            assert n[0] == step_at["table"], n[0]

            dve.wait_ge(S["x_early"], 16)
            dve.tensor_reduce(mx[0:P, 2:3], XE, AX.X, ALU.max)
            step(dve.tensor_reduce(bd[0:P, 0:1], XE, AX.X, ALU.min))
            step(dve.scalar_tensor_tensor(mx[0:P, 2:3], bd[0:P, 0:1], -1.0, mx[0:P, 2:3], ALU.mult, ALU.max), "max_ready")
            dve.wait_ge(S["tab_back"], 16)
            done = dve.alloc_register("dve_steps_done")
            chunk = dve.alloc_register("dve_chunk")
            dve.reg_mov(done, 0)
            regs = [dve.alloc_register("dve_first"), dve.alloc_register("dve_count")]
            with dve.Fori(0, NWIN) as w:
                dve.load(regs, TAB[0:1, bass.ds(w * 4, 2)])
                dve.reg_mov(chunk, regs[0])
                count = dve.snap(regs[1], min_val=1, max_val=EC // K)
                with dve.Fori(0, count) as _i:
                    c = dve.snap(chunk, min_val=0, max_val=EC - 1)
                    t = dve.snap(done, min_val=0, max_val=1 << 20)
                    slot = t & (RING - 1)
                    dve.wait_ge(S["hot_free"], t + 1)
                    rel = KR[:, bass.ds(slot * K, K)]
                    dve.tensor_scalar(rel, KEY[:, bass.ds(c, K)], WT[:, bass.ds(w, 1)], HALF,
                                      ALU.subtract, ALU.mult).then_inc(S["key_rel"], 1)
                    dve.tensor_tensor(LR[:, bass.ds(slot * (K * 128), P * K)].rearrange("p (a b) -> p a b", b=K),
                                      iotax[:, 0:P, :],
                                      LO[:, bass.ds(c, K)].rearrange("p (a b) -> p a b", a=1).broadcast_to([P, P, K]),
                                      ALU.is_equal).then_inc(S["hot_ready"], 1)
                    dve.wait_ge(S["key_rel"], t + 1)
                    dve.tensor_tensor(MR[:, bass.ds(slot * (K * WC), WC * K)].rearrange("p (a b) -> p a b", b=K),
                                      iotax,
                                      rel.rearrange("p (a b) -> p a b", a=1).broadcast_to([P, WC, K]),
                                      ALU.is_equal).then_inc(S["hot_ready"], 1)
                    dve.reg_add(done, done, 1)
                    dve.reg_add(chunk, chunk, K)

            dve.wait_ge(S["deg_mm"], 1)
            deg = ps[7][0:P, 0:NC]
            step(dve.tensor_scalar(s1, deg, 1.0, None, ALU.max))
            dve.reciprocal(s1, s1)
            dve.tensor_scalar(sd, deg, 1.0, None, ALU.add).then_inc(S["deg_plus"], 1)
            dve.wait_ge(S["deg_root"], 1)
            dve.reciprocal(dinv, sd)
            dve.wait_ge(S["max_done"], 1)
            dve.wait_ge(S["bounds_root"], 1)
            dve.tensor_copy(bd[:, 0:1], mx[:, 2:3])
            step(dve.tensor_tensor(bd[:, 1:2], sq[:, 0:1], sq[:, 1:2], ALU.add))
            step(dve.scalar_tensor_tensor(bd[:, 1:2], bd[:, 1:2], ROWB, mx[:, 0:1], ALU.mult, ALU.add))
            step(dve.scalar_tensor_tensor(bd[:, 2:3], sq[:, 2:3], ROWB, mx[:, 1:2], ALU.mult, ALU.add))
            step(dve.tensor_scalar(bd, bd, 2.0 ** -60, 2.0 ** 100, ALU.max, ALU.min))
            bi, sci, sii = bd.bitcast(I32), sc.bitcast(I32), si.bitcast(I32)
            step(dve.tensor_scalar(bi, bi, 23, None, ALU.logical_shift_right))
            step(dve.tensor_copy(sc, bi))
            dve.tensor_scalar(si, sc, -14.0, None, ALU.add)
            step(dve.tensor_scalar(sc, sc, -1.0, 268.0, ALU.mult, ALU.add))
            step(dve.tensor_copy(bi, sc))
            step(dve.tensor_scalar(sci, bi, 23, None, ALU.logical_shift_left))
            step(dve.tensor_copy(bi, si))
            step(dve.tensor_scalar(sii, bi, 23, None, ALU.logical_shift_left), "scales_ready")

            def wait(name, v):
                if v:
                    dve.wait_ge(S[name], v)

            def evac(s, b):
                kind = STAGES[s][0]
                if kind not in ("gcn0", "gcn1", "gcn2"):
                    return
                o_, m = cols(b)
                wait("agg_done", val("agg_done", s, b))
                wait("dense_done", before("dense_done", s, b))
                wait("xt_ready", val("xt_ready", s - 1, b))
                agg = ps[val("agg_done", s, b) % 2][:, 0:m]
                scale = {"gcn0": si[:, 0:1], "gcn1": 1.0 / SCALE, "gcn2": si[:, 2:3]}[kind]
                made["ag_ready"] = made.get("ag_ready", 0) + 1
                dve.scalar_tensor_tensor(AG[:, 0:m], agg, scale, XT[:, o_:o_ + m], ALU.mult,
                                         ALU.add).then_inc(S["ag_ready"], 1)

            def each(m, fn, name=None):
                for j in range(m):
                    ins = fn(j)
                step(ins, name)

            def norm(s, b, v, m, name=None):
                each(m, lambda j: dve.bn_stats(st[:, j, :], v[:, j, :]))
                each(m, lambda j: dve.bn_aggr(mv[:, j, :], st[:, j, :]))
                step(dve.tensor_scalar(rs[:, 0:m], mv[:, 0:m, 1], EPS, None, ALU.add), "var_ready")
                wait("sd_ready", val("sd_ready", s, b))
                step(dve.reciprocal(rs[:, 0:m], rs[:, 0:m]))
                each(m, lambda j: dve.tensor_scalar(v[:, j, :], v[:, j, :], mv[:, j, 0:1], rs[:, j:j + 1],
                                                    ALU.subtract, ALU.mult), name)

            def split2(v, cs, out, scale=SCALE):
                step(dve.tensor_scalar(out[0][:, cs, :], v, scale, None, ALU.mult))
                step(dve.scalar_tensor_tensor(out[1][:, cs, :], v, scale, out[0][:, cs, :], ALU.mult,
                                              ALU.subtract), "parts_done")

            def elem(s, b):
                kind, pin, pout = STAGES[s]
                m = chunks_of(b)
                c0 = CPB * b
                cs = slice(c0, c0 + m)
                u, t = U2[b % 2][:, 0:m, :], T[:, 0:m, :]
                d0 = ps[2][0:P, 0:m * D].rearrange("p (c f) -> p c f", f=D)
                d1 = ps[3][0:P, 0:m * D].rearrange("p (c f) -> p c f", f=D)
                bb = BB.rearrange("p (a f) -> p a f", a=1).broadcast_to([P, m, D])

                def own(v, j):
                    return v[:, c0 + j:c0 + j + 1]

                if not kind.startswith("gru"):
                    if b >= 2:
                        wait("tf_done", plan.get(("tf_done", s, b - 2)))
                        for i in (f"x2_stored{b % 2}", f"out_stored{b % 2}"):
                            wait(i, plan.get((i, s, b - 2)))
                    else:
                        wait("tf_done", before("tf_done", s, 0))
                if kind == "prep":
                    wait("x_in", 16)
                    each(m, lambda j: dve.tensor_scalar(u[:, j, :], XALL[:, c0 + j, :], own(dinv, j), None, ALU.mult), "u_ready")
                    split2(u, cs, pout, sc[0:P, 0:1])
                    return
                wait("stage_w", val("stage_w", s))
                if not kind.startswith("gru"):
                    wait("dense_done", val("dense_done", s, b))
                if kind in ("gcn0", "gcn1"):
                    each(m, lambda j: dve.scalar_tensor_tensor(u[:, j, :], d0[:, j, :], own(dinv, j), BB,
                                                               ALU.mult, ALU.add), "dense_free")
                if kind == "gcn0":
                    step(dve.tensor_scalar(t, u, 0.0, ab[:, 0:1], ALU.min, ALU.mult))
                    step(dve.scalar_tensor_tensor(u, u, 0.0, t, ALU.max, ALU.add))
                    wait("rx_in", val("rx_in", s, b))
                    step(dve.tensor_tensor(u, u, RX[:, 0:m, :], ALU.add), "rx_free")
                    norm(s, b, u, m, "u_ready")
                    split2(u, cs, pout)
                if kind in ("sage1", "sage2"):
                    step(dve.tensor_tensor(u, d1, bb, ALU.add))
                    each(m, lambda j: dve.scalar_tensor_tensor(u[:, j, :], d0[:, j, :], own(s1, j), u[:, j, :],
                                                               ALU.mult, ALU.add), "dense_free")
                if kind == "sage1":
                    step(dve.tensor_scalar(u, u, 0.0, None, ALU.max), "u_ready")
                    split2(u, cs, pout, sc[0:P, 1:2])
                if kind == "sage2":
                    step(dve.tensor_tensor(t, PB[0][:, cs, :], PB[1][:, cs, :], ALU.add))
                    step(dve.scalar_tensor_tensor(u, t, 1.0 / SCALE, u, ALU.mult, ALU.add))
                    norm(s, b, u, m, "u_ready")
                    split2(u, cs, pout)
                if kind == "gcn1":
                    step(dve.scalar_tensor_tensor(u, u, 0.2, u, ALU.mult, ALU.max))
                    each(m, lambda j: dve.tensor_scalar(u[:, j, :], u[:, j, :], own(dinv, j), None, ALU.mult), "u_ready")
                    split2(u, cs, pout, sc[0:P, 2:3])
                if kind == "gcn2":
                    each(m, lambda j: dve.scalar_tensor_tensor(u[:, j, :], d0[:, j, :], own(dinv, j), WB[0:P],
                                                               ALU.mult, ALU.mult), "dense_free")
                    step(dve.tensor_tensor(u, u, bb, ALU.add))
                    step(dve.tensor_tensor(t, PB[0][:, cs, :], PB[1][:, cs, :], ALU.add))
                    step(dve.tensor_scalar(t, t, 1.0 / SCALE, None, ALU.mult))
                    each(m, lambda j: dve.scalar_tensor_tensor(u[:, j, :], t[:, j, :], own(sd, j), u[:, j, :],
                                                               ALU.mult, ALU.add))
                    norm(s, b, u, m, "u_ready")
                if kind.startswith("gru"):
                    o_, q = cols(b)
                    r, z, g_, nx = GR[:, 0:q], GZ[:, 0:q], GT[:, 0:q], NX[:, 0:q]
                    wait("r_ready", val("r_ready", s, b))
                    step(dve.scalar_tensor_tensor(r, ps[5][:, 0:q], gb[:, 5:6], r, ALU.add, ALU.mult))
                    wait("z_ready", val("z_ready", s, b))
                    step(dve.tensor_tensor(r, r, ps[4][:, 0:q], ALU.add), "pre_n")
                    wait("n_ready", val("n_ready", s, b))
                    step(dve.tensor_tensor(g_, XT[:, o_:o_ + q], r, ALU.subtract))
                    step(dve.tensor_tensor(g_, g_, z, ALU.mult))
                    wait("tn_done", before("tn_done", s, b))
                    wait("nx_copied", before("nx_copied", s, b))
                    step(dve.tensor_tensor(nx, r, g_, ALU.add), "nx_ready")
                    wait("tn_done", val("tn_done", s, b))
                    tn = ps[6][0:P, 0:m * D].rearrange("p (c f) -> p c f", f=D)
                    if kind == "gru":
                        split2(tn, cs, pout)
                    else:
                        wait("rx_in", val("rx_in", s, b))
                        y = Y[:, 0:m, :]
                        step(dve.scalar_tensor_tensor(y, y, 2.0, tn, ALU.mult, ALU.add), "tn_free")
                        norm(s, b, y, m)
                        each(m, lambda j: dve.tensor_scalar(y[:, j, :], y[:, j, :], own(dinv, j), None, ALU.mult), "u_ready")
                        split2(y, cs, pout)

            for s in range(NS):
                if STAGES[s][0] == "prep":
                    for b in range(NB):
                        elem(s, b)
                    continue
                evac(s, 0)
                for b in range(NB):
                    if b + 1 < NB:
                        evac(s, b + 1)
                    elem(s, b)

        @block.tensor
        def _(pe):
            pe.wait_ge(S["weights_in"], 16 * 18)
            pe.wait_ge(S["consts"], CONST_EARLY)
            for g in range(4):
                for k in range(4 * g, min(4 * g + 4, 14)):
                    i = pe.transpose(ps[g][:, (k % 4) * D:(k % 4 + 1) * D], WR[:, k * D:(k + 1) * D], ident)
                i.then_inc(S["weights_turned"], 1)
            pe.matmul(ps[7][0:1, 0:D], ctxc, WGB[:, 0:D], start=True, stop=True)
            pe.matmul(ps[7][0:1, D:2 * D], ctxc, WGB[:, D:2 * D], start=True, stop=True).then_inc(S["rows_mm"], 1)
            pe.wait_ge(S["turned_kept"], 4)
            for l in range(4):
                pe.matmul(ps[l][:, 0:3 * D], TW[:, (10 + l) * D:(11 + l) * D], TW[:, 4 * D:7 * D],
                          start=True, stop=True).then_inc(S["wc_mm"], 1)
            for g in range(4):
                if g == 0:
                    pe.wait_ge(S["dve_step"], step_at["keyd"])
                else:
                    pe.wait_ge(S["keys_kept"], g)
                what = dw if g < 2 else es
                for j in range(4):
                    jj = 4 * (g % 2) + j
                    i = pe.transpose(ps[6][0:P, j * EP:(j + 1) * EP], what[:, jj * P:(jj + 1) * P], ident[0:EP, 0:EP])
                i.then_inc(S["keys_turned"], 1)

            pe.wait_ge(S["tab_back"], 16)
            pe.wait_ge(S["wc_done"], 4)
            done = pe.alloc_register("pe_steps_done")
            pe.reg_mov(done, 0)
            pe.sem_inc(S["hot_free"], RING)
            regs = [pe.alloc_register("pe_first"), pe.alloc_register("pe_count")]

            def window(w, bank):
                pe.load(regs, TAB[0:1, bass.ds(w * 4, 2)])
                count = pe.snap(regs[1], min_val=1, max_val=EC // K)
                pe.wait_ge(S["win_kept"], w + 1)
                pe.matmul(ps[bank][:, 0:2], ZZ, ZZ[:, 0:2], start=True, stop=False, skip_group_check=True)
                with pe.Fori(0, count) as _i:
                    t = pe.snap(done, min_val=0, max_val=1 << 20)
                    slot = t & (RING - 1)
                    pe.wait_ge(S["hot_ready"], 2 * t + 2)
                    lo = LR[:, bass.ds(slot * (K * 128), 128 * K)].rearrange("p (a b) -> p a b", b=K)
                    mo = MR[:, bass.ds(slot * (K * WC), WC * K)].rearrange("p (a b) -> p a b", b=K)
                    for k in range(K):
                        i = pe.matmul(ps[bank][:, 0:WC], lo[:, :, k], mo[:, :, k], start=False, stop=False,
                                      skip_group_check=True)
                    i.then_inc(S["hot_free"], 1)
                    pe.reg_add(done, done, 1)
                pe.matmul(ps[bank][:, 0:2], ZZ, ZZ[:, 0:2], start=False, stop=True,
                          skip_group_check=True).then_inc(S["win_done"], 1)

            with pe.Fori(0, (NWIN - 1) // 2) as pair:
                window(pair * 2, 0)
                window(pair * 2 + 1, 1)
            window(NWIN - 1, 0)

            pe.wait_ge(S["deg_in"], 16)
            for c in range(NC):
                i = pe.matmul(ps[7][0:P, c:c + 1], DEGR[:, c * P:(c + 1) * P], ones[0:NC, 0:1], start=True, stop=True)
            i.then_inc(S["deg_mm"], 1)

            def wait(name, v):
                if v:
                    pe.wait_ge(S[name], v)

            def spmm(s, b):
                pin = STAGES[s][1]
                o_, m = cols(b)
                g = val("agg_done", s, b)
                if g > 2:
                    wait("ag_ready", g - 2)
                agg = ps[g % 2][:, 0:m]
                for k in range(NC):
                    if b == 0 and k % CPB == 0:
                        if k // CPB >= NB - 2 or s == 1:
                            turn(s - 1, k // CPB)
                        wait("parts_done", val("parts_done", s - 1, k // CPB))
                    for q, part in enumerate(pin):
                        i = pe.matmul(agg, part[:, k, :], AT[:, k, o_:o_ + m], start=k == 0 and q == 0,
                                      stop=k == NC - 1 and q == len(pin) - 1)
                i.then_inc(S["agg_done"], 1)

            def dense(s, b):
                kind = STAGES[s][0]
                o_, m = cols(b)
                if b == 0:
                    wait("stage_w", val("stage_w", s))
                wait("ag_ready", val("ag_ready", s, b))
                wait("dense_free", before("dense_free", s, b))
                wait("pre_n", before("pre_n", s, b))
                if kind.startswith("gru"):
                    xt = XT[:, o_:o_ + m]
                    if STAGES[s - 1][0] == "gru":
                        wait("nx_copied", val("nx_copied", s - 1, b))
                    else:
                        wait("xt_ready", val("xt_ready", s - 1, b))
                    for g in range(2):
                        pe.matmul(ps[2 + g][:, 0:m], WCG[:, g * D:(g + 1) * D], AG[:, 0:m], start=True, stop=False)
                        pe.matmul(ps[2 + g][:, 0:m], WHH[:, g * D:(g + 1) * D], xt, start=False, stop=True)
                    pe.matmul(ps[4][:, 0:m], WCG[:, 2 * D:3 * D], AG[:, 0:m], start=True, stop=True)
                    i = pe.matmul(ps[5][:, 0:m], WHH[:, 2 * D:3 * D], xt, start=True, stop=True)
                else:
                    if kind.startswith("sage"):
                        wait("xs_ready", val("xs_ready", s, b))
                    for j in range(chunks_of(b)):
                        i = pe.matmul(ps[2][0:P, j * D:(j + 1) * D], AG[:, j * P:(j + 1) * P], WA, start=True, stop=True)
                        if kind.startswith("sage"):
                            i = pe.matmul(ps[3][0:P, j * D:(j + 1) * D], XS[:, j * P:(j + 1) * P], WB, start=True, stop=True)
                i.then_inc(S["dense_done"], 1)

            def turn(s, b):
                kind = STAGES[s][0]
                if kind.startswith("gru"):
                    wait("nx_ready", val("nx_ready", s, b))
                    prev = (s, b - 1) if b else (s - 1, NB - 1)
                    if STAGES[prev[0]][0] == "gru":
                        wait("parts_done", val("parts_done", *prev))
                    elif b:
                        wait("tn_free", val("tn_free", *prev))
                    for j in range(chunks_of(b)):
                        i = pe.transpose(ps[6][0:P, j * D:(j + 1) * D], NX[:, j * P:(j + 1) * P], ident)
                    i.then_inc(S["tn_done"], 1)
                if ("u_ready", s, b) in plan and kind != "gcn2":
                    wait("u_ready", val("u_ready", s, b))
                    wait("xt_ready", before("xt_ready", s, b))
                    v = Y if kind == "gru_last" else U2[b % 2]
                    for j in range(chunks_of(b)):
                        i = pe.transpose(ps[7][:, j * P:(j + 1) * P], v[:, j, :], ident[0:P, 0:P])
                    i.then_inc(S["tf_done"], 1)

            for s in range(1, NS):
                spmm(s, 0)
                for b in range(NB):
                    if b + 1 < NB:
                        spmm(s, b + 1)
                    dense(s, b)
                    if 0 < b < NB - 1:
                        turn(s, b - 1)

        @block.scalar
        def _(act):
            for g in range(4):
                act.wait_ge(S["weights_turned"], g + 1)
                m = (4 if g < 3 else 2) * D
                act.activation(TW[:, 4 * g * D:4 * g * D + m], ps[g][:, 0:m], ACT.Copy).then_inc(S["turned_kept"], 1)
            for l in range(4):
                act.wait_ge(S["wc_mm"], l + 1)
                act.activation(WCT[:, 3 * D * l:3 * D * (l + 1)], ps[l][:, 0:3 * D], ACT.Copy).then_inc(S["wc_done"], 1)
            act.wait_ge(S["gate_pre"], 1)
            act.activation(row[:, 2 * D:3 * D], row[:, 2 * D:3 * D], ACT.Sigmoid).then_inc(S["gate_done"], 1)

            act.sem_inc(S["win_kept"], 2)

            def keep(w, bank, m):
                act.wait_ge(S["win_done"], w + 1)
                v = ps[bank][0:P + 1, 0:WC].rearrange("p (c d) -> p c d", d=W)[:, :, 0:m]
                act.activation(ATX[:, :, bass.ds(w * W, m)], v, ACT.Copy).then_inc(S["win_kept"], 1)

            with act.Fori(0, (NWIN - 1) // 2) as pair:
                keep(pair * 2, 0, W)
                keep(pair * 2 + 1, 1, W)
            keep(NWIN - 1, 0, LASTW)

            act.wait_ge(S["deg_plus"], 1)
            act.activation(sd, sd, ACT.Sqrt).then_inc(S["deg_root"], 1)
            act.wait_ge(S["sums_done"], 1)
            act.activation(sq, sq, ACT.Sqrt).then_inc(S["bounds_root"], 1)

            def wait(name, v):
                if v:
                    act.wait_ge(S[name], v)

            def evac(s, b):
                kind = STAGES[s][0]
                if kind not in ("sage1", "sage2", "gru", "gru_last"):
                    return
                o_, m = cols(b)
                wait("dense_done", before("dense_done", s, b))
                if kind.startswith("sage"):
                    if b == 0:
                        wait("rx_free", total["rx_free"])
                    wait("xt_ready", val("xt_ready", s - 1, b))
                    act.activation(XS[:, 0:m], XT[:, o_:o_ + m], ACT.Copy).then_inc(S["xs_ready"], 1)
                wait("agg_done", val("agg_done", s, b))
                agg = ps[val("agg_done", s, b) % 2][:, 0:m]
                scale = si[:, 1:2] if kind == "sage2" else 1.0 / SCALE
                wait("scales_ready", 1)
                act.activation(AG[:, 0:m], agg, ACT.Copy, scale=scale).then_inc(S["ag_ready"], 1)

            def keep_turned(s, b):
                if ("xt_ready", s, b) in plan:
                    o_, m = cols(b)
                    wait("tf_done", val("tf_done", s, b))
                    act.activation(XT[:, o_:o_ + m], ps[7][:, 0:m], ACT.Copy).then_inc(S["xt_ready"], 1)

            def gates(s, b):
                kind = STAGES[s][0]
                o_, q = cols(b)
                m = chunks_of(b)
                if kind.startswith("gru"):
                    wait("dense_done", val("dense_done", s, b))
                    wait("x2_stored0", total["x2_stored0"])
                    wait("x2_stored1", total["x2_stored1"])
                    wait("tf_done", before("tf_done", 4, 0))
                    wait("parts_done", before("parts_done", 4, 0))
                    wait("nx_ready", before("nx_ready", s, b))
                    act.activation(GR[:, 0:q], ps[2][:, 0:q], ACT.Sigmoid, bias=gb[:, 0:1]).then_inc(S["r_ready"], 1)
                    act.activation(GZ[:, 0:q], ps[3][:, 0:q], ACT.Sigmoid, bias=gb[:, 1:2]).then_inc(S["z_ready"], 1)
                    wait("pre_n", val("pre_n", s, b))
                    act.activation(GR[:, 0:q], GR[:, 0:q], ACT.Tanh, bias=gb[:, 2:3]).then_inc(S["n_ready"], 1)
                if kind == "gru":
                    wait("nx_ready", val("nx_ready", s, b))
                    act.activation(XT[:, o_:o_ + q], NX[:, 0:q], ACT.Copy).then_inc(S["nx_copied"], 1)
                if kind in ("gcn0", "sage2", "gru_last", "gcn2"):
                    wait("var_ready", val("var_ready", s, b))
                    act.activation(rs[:, 0:m], rs[:, 0:m], ACT.Sqrt).then_inc(S["sd_ready"], 1)

            for b in range(NB):
                keep_turned(0, b)
            for s in range(1, NS):
                evac(s, 0)
                for b in range(NB):
                    if b + 1 < NB:
                        evac(s, b + 1)
                    if 0 < b < NB - 1:
                        keep_turned(s, b - 1)
                    gates(s, b)
                keep_turned(s, NB - 2)
                keep_turned(s, NB - 1)


_INS = ['x', 'src', 'dst', 'L0_gnn_W', 'L0_gnn_b', 'L0_gnn_a', 'L1_gnn_W1_l', 'L1_gnn_b1', 'L1_gnn_W1_r',
        'L1_gnn_W2_l', 'L1_gnn_b2', 'L1_gnn_W2_r', 'L2_gnn_weight', 'L2_gnn_w_ih', 'L2_gnn_w_hh', 'L2_gnn_b_ih',
        'L2_gnn_b_hh', 'L3_gnn_ctx', 'L3_gnn_W1', 'L3_gnn_b1', 'L3_gnn_W2', 'L3_gnn_b2', 'L3_gnn_Wg', 'L3_gnn_bg',
        'L3_gnn_Wb']

_OUT = ((N, D), "float32")


def kernel(**inputs):
    import numpy as np
    import concourse.bacc as bacc
    from concourse.bass_utils import run_bass_kernel_spmd

    nc = bacc.Bacc("TRN2", target_bir_lowering=False, num_devices=1)
    arrays, args = {}, []
    for name in _INS:
        a = np.ascontiguousarray(inputs[name])
        if a.ndim == 0:
            a = a.reshape(1)
        arrays[f"in_{name}"] = a
        args.append(nc.dram_tensor(f"in_{name}", a.shape, mybir.dt.from_np(a.dtype), kind="ExternalInput").ap())
    out = nc.dram_tensor("out", _OUT[0], mybir.dt.from_np(np.dtype(_OUT[1])), kind="ExternalOutput").ap()
    build(nc, *args, out)
    r = run_bass_kernel_spmd(nc, [arrays], core_ids=[0])
    return r.results[0]["out"]
```

```python
from contextlib import ExitStack

import concourse.bass as bass
from concourse import mybir

F32 = mybir.dt.float32
F16 = mybir.dt.float16
BF16 = mybir.dt.bfloat16
I32 = mybir.dt.int32
ALU = mybir.AluOpType
ACT = mybir.ActivationFunctionType
AX = mybir.AxisListType

D = 128
P = 125
N = 3125
NC = N // P
E = 100000
EC = E // P
W = 16
WC = NC * W
NWIN = -(-N // W)
LASTW = N - (NWIN - 1) * W
K = 4
KH = K // 2
RR = 2
ECP = EC + K
WP = NWIN // 2
WQ = 14
EP, EJ = 100, 8
BIG = 1024.0
HALF = 0.5
ROUND = 12582912.0
CPB = 4
NB = -(-NC // CPB)
SCALE = 4096.0
ROWB = 11.5
EPS = 1e-5


def chunks_of(b):
    return min(CPB, NC - CPB * b)


def build(nc, x_d, src_d, dst_d, w0_d, b0_d, a_d, w1l_d, b1_d, w1r_d, w2l_d, b2_d, w2r_d,
          gw_d, wih_d, whh_d, bih_d, bhh_d, ctx_d, w31_d, b31_d, w32_d, b32_d, wg_d, bg_d, wb_d, out_d):
    cm_s = nc.dram_tensor("chunk_bounds", [2, EC], F32, kind="Internal").ap()
    tab_s = nc.dram_tensor("window_table", [WP * 4], I32, kind="Internal").ap()
    wt_s = nc.dram_tensor("weights_turned", [4, D, D], F32, kind="Internal").ap()
    whh_s = nc.dram_tensor("whh_turned", [D, 3 * D], F32, kind="Internal").ap()
    wc_s = nc.dram_tensor("gate_weights", [4, D, 3 * D], F32, kind="Internal").ap()
    rows_s = nc.dram_tensor("gate_rows", [2, D], F32, kind="Internal").ap()
    x2_s = nc.dram_tensor("x2", [N, D], F32, kind="Internal").ap()

    with ExitStack() as ctx:
        def sem(name):
            return ctx.enter_context(nc.semaphore(name))

        ATX = ctx.enter_context(nc.sbuf_tensor("counts", [P + 1, NC, N], F16))
        AT = ATX[0:P]
        ARENA = 56576
        arena = ctx.enter_context(nc.sbuf_tensor("arena", [128, ARENA // 4], F32))

        def at(off, count, dt=F32, parts=128):
            size = 2 if dt in (F16, BF16) else 4
            assert off % 4 == 0 and off + count * size <= ARENA, (off, count)
            words = -(-count * size // 4)
            v = arena[0:parts, off // 4:off // 4 + words]
            return (v if dt == F32 else v.bitcast(dt))[:, 0:count]

        O_XT, O_PA, O_PB, O_AG = 0, 12512, 31712, 44512
        O_XS, O_U, O_W = 46528, 48576, 50624
        O_ID, O_SM = 54208, 54720
        XT = at(O_XT, N)
        PA = [at(O_PA + 6400 * k, NC * D, F16, P).rearrange("p (c f) -> p c f", f=D) for k in range(2)]
        PB = [at(O_PB + 6400 * k, NC * D, F16, P).rearrange("p (c f) -> p c f", f=D) for k in range(2)]
        AG = at(O_AG, CPB * P)
        XS = at(O_XS, CPB * P)
        RX = at(O_XS, CPB * D, F32, P).rearrange("p (c f) -> p c f", f=D)
        U2 = [at(o, CPB * D, F32, P).rearrange("p (c f) -> p c f", f=D) for o in (O_U, O_PA + 12800)]
        XALL = at(O_PB, NC * D, F32, P).rearrange("p (c f) -> p c f", f=D)
        WA = at(O_W, D)
        WB = at(O_W + 512, D)
        BB = at(O_W + 1024, D, F32, P)
        T = at(O_W + 1536, CPB * D, F32, P).rearrange("p (c f) -> p c f", f=D)
        WCG = at(O_W, 3 * D)
        WHH = at(O_W + 1536, 3 * D)
        O_P3 = O_PA + 12800
        GR = at(O_XS, CPB * P)
        GZ = at(O_U, CPB * P)
        GT = at(O_P3, CPB * P)
        NX = at(O_P3 + 2000, CPB * P)
        Y = at(O_P3 + 4000, CPB * D, F32, P).rearrange("p (c f) -> p c f", f=D)
        ident = at(O_ID, D)
        o = O_SM
        small = {}
        for name, cnt in (("dinv", NC), ("s1", NC), ("sd", NC), ("mv", 2 * CPB), ("rs", CPB), ("ab", 1),
                          ("gb", 6), ("st", 6 * CPB), ("sq", 3), ("mx", 3), ("sc", 3), ("si", 3), ("bd", 3), ("bc", 2)):
            small[name] = at(o, cnt)
            o += cnt * 4
        dinv, s1, sd = (small[k][0:P] for k in ("dinv", "s1", "sd"))
        mv = small["mv"][0:P].rearrange("p (c t) -> p c t", t=2)
        st = small["st"][0:P].rearrange("p (c t) -> p c t", t=6)
        rs, ab = small["rs"][0:P], small["ab"][0:P]
        gb = small["gb"]
        sq, mx, sc, si, bd, bc = (small[k] for k in ("sq", "mx", "sc", "si", "bd", "bc"))
        ones = at(o, 2, F16, P)
        W31R = at(42496, D)
        SQT = at(43520, D)
        XE = at(10880, NC * D, F32, P)
        DEGR = at(0, N, F16, NC)

        iotax = at(0, WC * KH, F16, P).rearrange("p (n k) -> p n k", k=KH)
        KL = at(4000, 2 * ECP, F32, P).rearrange("p (t c) -> p t c", t=2)
        MR = at(10880, K * WC, F16, P).rearrange("p (h n k) -> p h n k", h=2, k=KH)
        LR = at(23680, K * 128, F16, P).rearrange("p (h n k) -> p h n k", h=2, k=KH)
        KR = at(27776, RR * 2 * K, F16, P)
        TOT = at(25728, 1, I32, 1)
        TOTF = at(25732, 1, F32, 1)
        CNTF = at(25736, NWIN, F32, 1)
        WT = at(27840, 2 * NWIN, F32, P).rearrange("p (t c) -> p t c", t=2)
        ZZ = at(29408, 128, F16, P)
        TAB = at(29664, WP * 4, I32, 1)
        ei = at(10880, EJ * P, I32, EP)
        ef = at(14880, EJ * P, F32, EP)
        eh = at(18880, EJ * P, F32, EP)
        es = at(22880, EJ * P, F32, EP)
        di = at(30400, EJ * P, I32, EP)
        df = at(34400, EJ * P, F32, EP)
        dw = at(38400, EJ * P, F32, EP)
        CM = at(42400, 2 * EJ, F32, EP)
        CB = at(30400, 2 * EC, F32, WP)
        CI = at(36800, EC, F32, WP)
        TMP = at(40000, EC, F32, WP)
        WID = at(43200, 2, F32, WP)
        WM = at(43208, 8, F32, WP)
        TBI = at(43240, 4, I32, WP)
        WR = at(O_AG, 14 * D)
        TW = at(0, 14 * D)
        WCT = at(10880, 12 * D)
        row = at(51680, 4 * D, F32, 1)
        ctxc = at(53728, 1, F32, 64)
        WGB = at(7216, 2 * D, F32, 64)

        ps = [ctx.enter_context(nc.psum_tensor(f"bank{i}", [128, 512], F32)) for i in range(8)]

        names = ("x_in x_early sums_ready max_ready deg_in sums_done max_done bounds_root scales_ready weights_in edges_in sources_in consts weights_turned turned_kept wc_mm wc_done wc_kept rows_mm gate_pre "
                 "gate_done rows_done rows_kept dve_step keys_turned keys_kept cm_stored cm_back tab_stored "
                 "tab_back keys_made key_rel hot_made hot_ready hot_free win_done win_kept deg_mm deg_plus deg_root stage_w rx_in "
                 "rx_free parts_done agg_done ag_ready dense_done dense_free xs_ready xt_ready u_ready tn_done "
                 "tn_free tf_done sd_ready var_ready r_ready z_ready pre_n n_ready nx_ready nx_copied x2_stored0 "
                 "x2_stored1 out_stored0 out_stored1").split()
        S = {n: sem(n) for n in names}
        block = ctx.enter_context(nc.Block())

        STAGES = [("prep", None, PA), ("gcn0", PA, PB), ("sage1", PB, PA), ("sage2", PA, PB),
                  ("gru", PB, PA), ("gru", PA, PB), ("gru", PB, PA),
                  ("gru_last", PA, PB), ("gcn1", PB, PA), ("gcn2", PA, None)]
        NS = len(STAGES)
        gru_no = {4: 0, 5: 1, 6: 2, 7: 3}

        def cols(b):
            return P * b * CPB, P * chunks_of(b)

        plan = {}
        total = {}

        def event(name, key, inc=1):
            total[name] = total.get(name, 0) + inc
            plan[(name,) + key] = total[name]

        for s, (kind, pin, pout) in enumerate(STAGES):
            if kind != "prep":
                event("stage_w", (s,), 16 * {"gcn0": 2, "sage1": 3, "sage2": 3, "gru": 2, "gru_last": 2, "gcn1": 2, "gcn2": 3}[kind])
            for b in range(NB):
                k = (s, b)
                own = []
                if kind in ("gcn0", "gru_last"):
                    event("rx_in", k, 16)
                if kind == "gcn0":
                    own += ["rx_free"]
                if kind != "prep":
                    own += ["agg_done", "ag_ready", "dense_done"]
                if kind in ("gcn0", "sage1", "sage2", "gcn1", "gcn2"):
                    own += ["dense_free", "u_ready"]
                if kind in ("prep", "gru_last"):
                    own += ["u_ready"]
                if kind.startswith("sage"):
                    own += ["xs_ready"]
                if kind not in ("gru", "gcn2"):
                    own += ["tf_done", "xt_ready"]
                if kind.startswith("gru"):
                    own += ["r_ready", "z_ready", "pre_n", "n_ready", "nx_ready", "tn_done"]
                if kind == "gru":
                    own += ["nx_copied"]
                if kind == "gru_last":
                    own += ["tn_free"]
                if kind in ("gcn0", "sage2", "gru_last", "gcn2"):
                    own += ["var_ready", "sd_ready"]
                if pout is not None:
                    own += ["parts_done"]
                for n in own:
                    event(n, k)
                if kind == "sage2":
                    event(f"x2_stored{b % 2}", k, 16)
                if kind == "gcn2":
                    event(f"out_stored{b % 2}", k, 16)

        def val(name, s, b=None):
            return plan[(name, s) if b is None else (name, s, b)]

        def before(name, s, b):
            keys = [(name, t, c) for t in range(s + 1) for c in range(NB) if (t, c) < (s, b)]
            for k in reversed(keys):
                if k in plan:
                    return plan[k]
            return None

        step_at = {"bounds": 7, "keyd": 15, "table": 37}

        @block.sync
        def _(sp):
            for k, w in enumerate((w1l_d, w1r_d, w2l_d, w2r_d)):
                sp.dma_start(WR[:, k * D:(k + 1) * D], w).then_inc(S["weights_in"], 16)
            sp.dma_start(WR[:, 4 * D:7 * D].rearrange("p (g i) -> p g i", g=3),
                         wih_d.rearrange("(g p) i -> p g i", p=D)).then_inc(S["weights_in"], 16)
            sp.dma_start(WR[:, 7 * D:10 * D].rearrange("p (g i) -> p g i", g=3),
                         whh_d.rearrange("(g p) i -> p g i", p=D)).then_inc(S["weights_in"], 16)
            sp.dma_start(WR[:, 10 * D:14 * D].rearrange("p (l i) -> p l i", l=4),
                         gw_d.rearrange("l p i -> p l i")).then_inc(S["weights_in"], 16)
            sp.dma_start(WGB[:, 0:D], wg_d).then_inc(S["weights_in"], 16)
            sp.dma_start(WGB[:, D:2 * D], wb_d).then_inc(S["weights_in"], 16)
            sp.dma_start(ctxc, ctx_d.rearrange("a k -> k a")).then_inc(S["weights_in"], 16)
            sp.dma_start(W31R, w31_d).then_inc(S["weights_in"], 16)
            sp.dma_start(bc[:, 0:1], b1_d.rearrange("(p a) -> p a", a=1)).then_inc(S["weights_in"], 16)
            sp.dma_start(bc[:, 1:2], b31_d.rearrange("(p a) -> p a", a=1)).then_inc(S["weights_in"], 16)
            sp.dma_start(row[:, 0:D], bg_d.rearrange("(a k) -> a k", a=1)).then_inc(S["weights_in"], 16)
            sp.dma_start(row[:, D:2 * D], b32_d.rearrange("(a k) -> a k", a=1)).then_inc(S["weights_in"], 16)
            sp.dma_start(di, dst_d.rearrange("(p f) -> p f", p=EP)).then_inc(S["edges_in"], 16)
            sp.dma_start(gb[:, 0:3], bih_d.rearrange("(g p) -> p g", p=D), allow_slow_non_contiguous=True).then_inc(S["weights_in"], 16)
            sp.dma_start(gb[:, 3:6], bhh_d.rearrange("(g p) -> p g", p=D), allow_slow_non_contiguous=True).then_inc(S["weights_in"], 16)
            sp.dma_start(ab, a_d.rearrange("(a b) -> a b", a=1).to_broadcast([P, 1])).then_inc(S["weights_in"], 16)
            sp.wait_ge(S["turned_kept"], 4)
            sp.dma_start(wt_s.rearrange("k p i -> p k i"),
                         TW[:, 0:4 * D].rearrange("p (k i) -> p k i", k=4)).then_inc(S["wc_kept"], 16)
            sp.dma_start(whh_s, TW[:, 7 * D:10 * D]).then_inc(S["wc_kept"], 16)
            sp.wait_ge(S["wc_done"], 4)
            sp.dma_start(wc_s.rearrange("l p i -> p l i"),
                         WCT.rearrange("p (l i) -> p l i", l=4)).then_inc(S["wc_kept"], 16)
            sp.wait_ge(S["wc_kept"], 48)
            sp.dma_start(ei, src_d.rearrange("(p f) -> p f", p=EP)).then_inc(S["sources_in"], 16)
            sp.wait_ge(S["rows_done"], 1)
            sp.dma_start(rows_s, row[:, 2 * D:4 * D]).then_inc(S["rows_kept"], 16)
            sp.wait_ge(S["dve_step"], step_at["bounds"])
            sp.dma_start(cm_s.rearrange("t (p j) -> p t j", p=EP),
                         CM.rearrange("p (t j) -> p t j", t=2)).then_inc(S["cm_stored"], 16)
            sp.wait_ge(S["cm_stored"], 16)
            sp.wait_ge(S["keys_kept"], 4)
            sp.dma_start(XE.rearrange("p (c f) -> p c f", f=D), x_d.rearrange("(c p) f -> p c f", p=P)).then_inc(S["x_early"], 16)
            for t in range(2):
                sp.dma_start(CB[:, t * EC:(t + 1) * EC], cm_s[t:t + 1, :].to_broadcast([WP, EC])).then_inc(S["cm_back"], 16)
            sp.wait_ge(S["dve_step"], step_at["table"])
            sp.dma_start(tab_s.rearrange("(p k) -> p k", p=WP), TBI).then_inc(S["tab_stored"], 16)
            sp.wait_ge(S["tab_stored"], 16)
            sp.dma_start(TAB, tab_s.rearrange("(a k) -> a k", a=1)).then_inc(S["tab_back"], 16)
            sp.dma_start(XALL, x_d.rearrange("(c p) f -> p c f", p=P)).then_inc(S["x_in"], 16)
            sp.wait_ge(S["rows_kept"], 16)
            sp.wait_ge(S["win_kept"], 2 + NWIN)
            sp.wait_ge(S["hot_made"], 1)
            sp.wait_ge(S["keys_made"], 1)
            sp.dma_start(DEGR, ATX[P:P + 1].rearrange("p c d -> p (c d)")).then_inc(S["deg_in"], 16)

            xv = x_d.rearrange("(c p) f -> p c f", p=P)
            x2v = x2_s.rearrange("(c p) f -> p c f", p=P)
            ov = out_d.rearrange("(c p) f -> p c f", p=P)
            for s, (kind, pin, pout) in enumerate(STAGES):
                if kind != "prep":
                    v = before("dense_done", s, 0)
                    if v:
                        sp.wait_ge(S["dense_done"], v)
                    v = before("parts_done", s, 0)
                    if v:
                        sp.wait_ge(S["parts_done"], v)
                q = S["stage_w"]
                if kind == "gcn0":
                    sp.dma_start(WA, w0_d).then_inc(q, 16)
                    sp.dma_start(BB, b0_d.rearrange("(a k) -> a k", a=1).to_broadcast([P, D])).then_inc(q, 16)
                if kind in ("sage1", "sage2"):
                    k = 0 if kind == "sage1" else 2
                    sp.dma_start(WA, wt_s[k]).then_inc(q, 16)
                    sp.dma_start(WB, wt_s[k + 1]).then_inc(q, 16)
                    bias = b1_d if kind == "sage1" else b2_d
                    sp.dma_start(BB, bias.rearrange("(a k) -> a k", a=1).to_broadcast([P, D])).then_inc(q, 16)
                if kind.startswith("gru"):
                    sp.dma_start(WCG, wc_s[gru_no[s]]).then_inc(q, 16)
                    sp.dma_start(WHH, whh_s).then_inc(q, 16)
                if kind == "gcn1":
                    sp.dma_start(WA, w31_d).then_inc(q, 16)
                    sp.dma_start(BB, b31_d.rearrange("(a k) -> a k", a=1).to_broadcast([P, D])).then_inc(q, 16)
                if kind == "gcn2":
                    sp.dma_start(WA, w32_d).then_inc(q, 16)
                    sp.dma_start(WB[0:P], rows_s[0:1, :].to_broadcast([P, D])).then_inc(q, 16)
                    sp.dma_start(BB, rows_s[1:2, :].to_broadcast([P, D])).then_inc(q, 16)
                for b in range(NB):
                    n = chunks_of(b)
                    cs = slice(CPB * b, CPB * b + n)
                    if kind in ("gcn0", "gru_last"):
                        if kind == "gcn0" and b:
                            sp.wait_ge(S["rx_free"], val("rx_free", s, b - 1))
                        if kind == "gru_last" and b:
                            sp.wait_ge(S["parts_done"], val("parts_done", s, b - 1))
                            sp.wait_ge(S["tf_done"], val("tf_done", s, b - 1))
                        if kind == "gru_last" and b == 0:
                            for i in ("x2_stored0", "x2_stored1"):
                                sp.wait_ge(S[i], total[i])
                        to = Y if kind == "gru_last" else RX
                        frm = x2v if kind == "gru_last" else xv
                        sp.dma_start(to[:, 0:n, :], frm[:, cs, :]).then_inc(S["rx_in"], 16)
                    if kind == "sage2":
                        sp.wait_ge(S["u_ready"], val("u_ready", s, b))
                        sp.dma_start(x2v[:, cs, :], U2[b % 2][:, 0:n, :]).then_inc(S[f"x2_stored{b % 2}"], 16)
                    if kind == "gcn2":
                        sp.wait_ge(S["u_ready"], val("u_ready", s, b))
                        sp.dma_start(ov[:, cs, :], U2[b % 2][:, 0:n, :]).then_inc(S[f"out_stored{b % 2}"], 16)
            for i in ("out_stored0", "out_stored1"):
                sp.wait_ge(S[i], total[i])

        @block.gpsimd
        def _(pool):
            pool.memset(ident, 0.0).then_inc(S["consts"], 1)
            pool.wait_ge(S["consts"], 1)
            pool.affine_select(out=ident, in_=ident, compare_op=ALU.not_equal, fill=1.0, base=0,
                               pattern=[[-1, D]], channel_multiplier=1).then_inc(S["consts"], 1)
            pool.iota(WT[:, 0, :], [[WC // 2, NWIN]], base=0, channel_multiplier=0,
                      allow_small_or_imprecise_dtypes=True).then_inc(S["consts"], 1)
            pool.memset(WT[:, 1, :], 0.0).then_inc(S["consts"], 1)
            pool.memset(ZZ, 0.0).then_inc(S["consts"], 1)
            pool.memset(ones, 1.0 / HALF).then_inc(S["consts"], 1)
            pool.wait_ge(S["wc_kept"], 48)
            pool.iota(iotax, [[1, WC], [0, KH]], base=0, channel_multiplier=0,
                      allow_small_or_imprecise_dtypes=True).then_inc(S["consts"], 1)
            pool.wait_ge(S["rows_mm"], 1)
            pool.memset(KL[:, :, EC:ECP], -1.0).then_inc(S["consts"], 1)
            pool.wait_ge(S["keys_turned"], 4)
            pool.memset(LR[:, :, P:P + 1, :], 1.0).then_inc(S["consts"], 1)
            pool.memset(LR[:, :, P + 1:128, :], 0.0).then_inc(S["consts"], 1)
            pool.wait_ge(S["dve_step"], step_at["bounds"])
            pool.iota(CI, [[1, EC]], base=0, channel_multiplier=0,
                      allow_small_or_imprecise_dtypes=True).then_inc(S["consts"], 1)
            pool.iota(WID, [[1, 2]], base=0, channel_multiplier=2,
                      allow_small_or_imprecise_dtypes=True).then_inc(S["consts"], 1)
            pool.wait_ge(S["sums_ready"], 1)
            pool.partition_all_reduce(sq, sq, 128, bass.bass_isa.ReduceOp.add).then_inc(S["sums_done"], 1)
            pool.wait_ge(S["max_ready"], 1)
            pool.partition_all_reduce(mx, mx, 128, bass.bass_isa.ReduceOp.max).then_inc(S["max_done"], 1)

            pool.wait_ge(S["tab_back"], 16)
            pool.wait_ge(S["keys_kept"], 4)
            pool.sem_inc(S["hot_ready"], 4 * RR)
            done = pool.alloc_register("pool_steps_done")
            chunk = pool.alloc_register("pool_chunk")
            pool.reg_mov(done, 0)
            regs = [pool.alloc_register(f"pool_{what}{q}") for q in range(WQ) for what in ("first", "count")]

            def rel_keys(c, w):
                t = pool.snap(done, min_val=0, max_val=1 << 20)
                slot = t & (RR - 1)
                pool.wait_ge(S["hot_ready"], t * 4 + 4)
                pool.tensor_tensor(KR[:, bass.ds(slot * (2 * K), 2 * K)].rearrange("p (t k) -> p t k", t=2),
                                   KL[:, :, bass.ds(c, K)], WT[:, :, bass.ds(w, 1)].broadcast_to([P, 2, K]),
                                   ALU.subtract).then_inc(S["key_rel"], 1)
                pool.reg_add(done, done, 1)

            with pool.Fori(0, NWIN // WQ) as quad:
                pool.load(regs, TAB[0:1, bass.ds(quad * (2 * WQ), 2 * WQ)])
                for q in range(WQ):
                    pool.reg_mov(chunk, regs[2 * q])
                    count = pool.snap(regs[2 * q + 1], min_val=1, max_val=EC // K)
                    with pool.Fori(0, count) as _i:
                        rel_keys(pool.snap(chunk, min_val=0, max_val=EC - 1), quad * WQ + q)
                        pool.reg_add(chunk, chunk, K)
            rel_keys(0, 0)
            pool.memset(CNTF[:, 1:2], 0.0).then_inc(S["keys_made"], 1)

        CONST_EARLY, CONST_IOTAX, CONST_ALL = 6, 7, 12

        @block.vector
        def _(dve):
            n = [0]
            made = {}

            def step(ins, name=None):
                if name is None:
                    n[0] += 1
                    ins.then_inc(S["dve_step"], 1)
                    dve.wait_ge(S["dve_step"], n[0])
                else:
                    made[name] = made.get(name, 0) + 1
                    ins.then_inc(S[name], 1)
                    dve.wait_ge(S[name], made[name])

            dve.wait_ge(S["edges_in"], 16)
            step(dve.tensor_copy(df, di))
            step(dve.tensor_scalar(dw, df, 1.0 / W, -0.5 + 0.5 / W, ALU.mult, ALU.add))
            step(dve.tensor_scalar(dw, dw, ROUND, None, ALU.add))
            step(dve.tensor_scalar(dw, dw, ROUND, None, ALU.subtract))
            dwv = dw.rearrange("p (j i) -> p j i", j=EJ)
            dve.tensor_reduce(CM[:, 0:EJ], dwv, AX.X, ALU.max)
            step(dve.tensor_reduce(CM[:, EJ:2 * EJ], dwv, AX.X, ALU.min))
            step(dve.scalar_tensor_tensor(df, dw, float(WC - W), df, ALU.mult, ALU.add))
            step(dve.tensor_copy(dw, df))
            assert n[0] == step_at["bounds"]
            dve.wait_ge(S["rows_mm"], 1)
            dve.tensor_tensor(row[:, 2 * D:3 * D], ps[7][0:1, 0:D], row[:, 0:D], ALU.add).then_inc(S["gate_pre"], 1)
            dve.tensor_tensor(gb[:, 0:2], gb[:, 0:2], gb[:, 3:5], ALU.add)
            dve.wait_ge(S["weights_in"], 16 * 18)
            for j, w in enumerate((WR[:, 0:D], WR[:, D:2 * D], W31R)):
                step(dve.tensor_tensor_reduce(SQT, w, w, 1.0, 0.0, ALU.mult, ALU.add, sq[:, j:j + 1]),
                     None if j < 2 else "sums_ready")
            dve.scalar_tensor_tensor(mx[:, 0:2], bc, -1.0, bc, ALU.mult, ALU.max)
            dve.memset(mx[:, 2:3], 0.0)
            dve.wait_ge(S["sources_in"], 16)
            step(dve.tensor_copy(ef, ei))
            step(dve.tensor_scalar(eh, ef, 1.0 / P, -0.5 + 0.5 / P, ALU.mult, ALU.add))
            step(dve.tensor_scalar(eh, eh, ROUND, None, ALU.add))
            step(dve.tensor_scalar(eh, eh, ROUND, None, ALU.subtract))
            step(dve.scalar_tensor_tensor(es, eh, -float(P), ef, ALU.mult, ALU.add))
            step(dve.scalar_tensor_tensor(dw, eh, float(W), dw, ALU.mult, ALU.add))
            assert n[0] == step_at["keyd"]
            dve.wait_ge(S["gate_done"], 1)
            step(dve.tensor_tensor(row[:, 3 * D:4 * D], row[:, 2 * D:3 * D], row[:, D:2 * D], ALU.mult))
            dve.tensor_tensor(row[:, 3 * D:4 * D], row[:, 3 * D:4 * D], ps[7][0:1, D:2 * D],
                              ALU.add).then_inc(S["rows_done"], 1)
            for g in range(4):
                dve.wait_ge(S["keys_turned"], g + 1)
                to = KL[:, g // 2, 0:EC].rearrange("p (c j) -> p j c", j=EJ)[:, 4 * (g % 2):4 * (g % 2) + 4, :]
                if g == 0:
                    dve.wait_ge(S["rows_mm"], 1)
                if g == 0:
                    dve.wait_ge(S["wc_kept"], 48)
                dve.tensor_scalar(to, ps[6][0:P, 0:4 * EP].rearrange("p (j c) -> p j c", j=4),
                                  HALF, None, ALU.mult).then_inc(S["keys_kept"], 1)
            dve.wait_ge(S["consts"], CONST_IOTAX)
            step(dve.tensor_scalar(iotax, iotax, HALF, None, ALU.mult))
            dve.wait_ge(S["cm_back"], 32)
            dve.wait_ge(S["consts"], CONST_ALL)
            for q in range(2):
                step(dve.tensor_scalar(TMP, CI, -1.0, BIG, ALU.mult, ALU.add))
                step(dve.scalar_tensor_tensor(TMP, CB[:, 0:EC], WID[:, q:q + 1], TMP, ALU.is_ge, ALU.mult))
                step(dve.tensor_reduce(WM[:, q:q + 1], TMP, AX.X, ALU.max))
                step(dve.tensor_scalar(TMP, CI, 1.0, None, ALU.add))
                step(dve.scalar_tensor_tensor(TMP, CB[:, EC:2 * EC], WID[:, q:q + 1], TMP, ALU.is_le, ALU.mult))
                step(dve.tensor_reduce(WM[:, 2 + q:3 + q], TMP, AX.X, ALU.max))
            step(dve.tensor_scalar(WM[:, 0:2], WM[:, 0:2], -1.0, BIG, ALU.mult, ALU.add))
            step(dve.tensor_scalar(WM[:, 0:2], WM[:, 0:2], float(EC - 1), None, ALU.min))
            step(dve.tensor_tensor(WM[:, 4:6], WM[:, 2:4], WM[:, 0:2], ALU.subtract))
            step(dve.tensor_scalar(WM[:, 4:6], WM[:, 4:6], 1.0 / K, 0.5 - 0.5 / K, ALU.mult, ALU.add))
            tb = TBI.rearrange("p (q k) -> p q k", q=2)
            step(dve.tensor_scalar(WM[:, 4:6], WM[:, 4:6], ROUND, None, ALU.add))
            step(dve.tensor_scalar(WM[:, 4:6], WM[:, 4:6], ROUND, None, ALU.subtract))
            step(dve.tensor_scalar(WM[:, 4:6], WM[:, 4:6], 1.0, None, ALU.max))
            dve.tensor_copy(tb[:, :, 0:1], WM[:, 0:2].rearrange("p (q k) -> p q k", k=1))
            step(dve.tensor_copy(tb[:, :, 1:2], WM[:, 4:6].rearrange("p (q k) -> p q k", k=1)))
            assert n[0] == step_at["table"], n[0]

            dve.wait_ge(S["x_early"], 16)
            dve.tensor_reduce(mx[0:P, 2:3], XE, AX.X, ALU.max)
            step(dve.tensor_reduce(bd[0:P, 0:1], XE, AX.X, ALU.min))
            step(dve.scalar_tensor_tensor(mx[0:P, 2:3], bd[0:P, 0:1], -1.0, mx[0:P, 2:3], ALU.mult, ALU.max), "max_ready")
            dve.wait_ge(S["tab_back"], 16)
            step(dve.tensor_copy(CNTF, TAB.rearrange("p (w k) -> p w k", k=2)[:, :, 1:2]))
            step(dve.tensor_reduce(TOTF, CNTF, AX.X, ALU.add))
            step(dve.tensor_scalar(TOTF, TOTF, 0.5, 0.25, ALU.mult, ALU.add))
            step(dve.tensor_scalar(TOTF, TOTF, ROUND, None, ALU.add))
            step(dve.tensor_scalar(TOTF, TOTF, ROUND, None, ALU.subtract))
            step(dve.tensor_copy(TOT, TOTF))
            pairs = dve.alloc_register("dve_pairs")
            dve.load(pairs, TOT)
            with dve.Fori(0, dve.snap(pairs, min_val=1, max_val=NWIN * EC // K)) as i:
                for r in range(RR):
                    dve.wait_ge(S["key_rel"], i * RR + (r + 1))
                    for h in range(2):
                        dve.wait_ge(S["hot_free"], i * (2 * RR) + (2 * r + h + 1))
                        rel = KR[:, r * 2 * K:(r + 1) * 2 * K].rearrange("p (t k) -> p t k", t=2)
                        dve.tensor_tensor(LR[:, h, 0:P, :], iotax[:, 0:P, :],
                                          rel[:, 1:2, h * KH:(h + 1) * KH].broadcast_to([P, P, KH]),
                                          ALU.is_equal).then_inc(S["hot_ready"], 1)
                        dve.tensor_tensor(MR[:, h], iotax, rel[:, 0:1, h * KH:(h + 1) * KH].broadcast_to([P, WC, KH]),
                                          ALU.is_equal).then_inc(S["hot_ready"], 1)

            dve.memset(CNTF[:, 0:1], 0.0).then_inc(S["hot_made"], 1)

            dve.wait_ge(S["keys_made"], 1)
            dve.wait_ge(S["deg_mm"], 1)
            deg = ps[7][0:P, 0:NC]
            step(dve.tensor_scalar(s1, deg, 1.0, None, ALU.max))
            dve.reciprocal(s1, s1)
            dve.tensor_scalar(sd, deg, 1.0, None, ALU.add).then_inc(S["deg_plus"], 1)
            dve.wait_ge(S["deg_root"], 1)
            dve.reciprocal(dinv, sd)
            dve.wait_ge(S["max_done"], 1)
            dve.wait_ge(S["bounds_root"], 1)
            dve.tensor_copy(bd[:, 0:1], mx[:, 2:3])
            step(dve.tensor_tensor(bd[:, 1:2], sq[:, 0:1], sq[:, 1:2], ALU.add))
            step(dve.scalar_tensor_tensor(bd[:, 1:2], bd[:, 1:2], ROWB, mx[:, 0:1], ALU.mult, ALU.add))
            step(dve.scalar_tensor_tensor(bd[:, 2:3], sq[:, 2:3], ROWB, mx[:, 1:2], ALU.mult, ALU.add))
            step(dve.tensor_scalar(bd, bd, 2.0 ** -60, 2.0 ** 100, ALU.max, ALU.min))
            bi, sci, sii = bd.bitcast(I32), sc.bitcast(I32), si.bitcast(I32)
            step(dve.tensor_scalar(bi, bi, 23, None, ALU.logical_shift_right))
            step(dve.tensor_copy(sc, bi))
            dve.tensor_scalar(si, sc, -13.0, None, ALU.add)
            step(dve.tensor_scalar(sc, sc, -1.0, 268.0, ALU.mult, ALU.add))
            step(dve.tensor_copy(bi, sc))
            step(dve.tensor_scalar(sci, bi, 23, None, ALU.logical_shift_left))
            step(dve.tensor_copy(bi, si))
            step(dve.tensor_scalar(sii, bi, 23, None, ALU.logical_shift_left), "scales_ready")

            def wait(name, v):
                if v:
                    dve.wait_ge(S[name], v)

            def evac(s, b):
                kind = STAGES[s][0]
                if kind not in ("gcn0", "gcn1", "gcn2"):
                    return
                o_, m = cols(b)
                wait("agg_done", val("agg_done", s, b))
                wait("dense_done", before("dense_done", s, b))
                wait("xt_ready", val("xt_ready", s - 1, b))
                agg = ps[val("agg_done", s, b) % 2][:, 0:m]
                scale = {"gcn0": si[:, 0:1], "gcn1": 1.0 / (SCALE * HALF), "gcn2": si[:, 2:3]}[kind]
                made["ag_ready"] = made.get("ag_ready", 0) + 1
                dve.scalar_tensor_tensor(AG[:, 0:m], agg, scale, XT[:, o_:o_ + m], ALU.mult,
                                         ALU.add).then_inc(S["ag_ready"], 1)

            def each(m, fn, name=None):
                for j in range(m):
                    ins = fn(j)
                step(ins, name)

            def norm(s, b, v, m, name=None):
                each(m, lambda j: dve.bn_stats(st[:, j, :], v[:, j, :]))
                each(m, lambda j: dve.bn_aggr(mv[:, j, :], st[:, j, :]))
                step(dve.tensor_scalar(rs[:, 0:m], mv[:, 0:m, 1], EPS, None, ALU.add), "var_ready")
                wait("sd_ready", val("sd_ready", s, b))
                step(dve.reciprocal(rs[:, 0:m], rs[:, 0:m]))
                each(m, lambda j: dve.tensor_scalar(v[:, j, :], v[:, j, :], mv[:, j, 0:1], rs[:, j:j + 1],
                                                    ALU.subtract, ALU.mult), name)

            def split2(v, cs, out, scale=SCALE):
                step(dve.tensor_scalar(out[0][:, cs, :], v, scale, None, ALU.mult))
                step(dve.scalar_tensor_tensor(out[1][:, cs, :], v, scale, out[0][:, cs, :], ALU.mult,
                                              ALU.subtract), "parts_done")

            def elem(s, b):
                kind, pin, pout = STAGES[s]
                m = chunks_of(b)
                c0 = CPB * b
                cs = slice(c0, c0 + m)
                u, t = U2[b % 2][:, 0:m, :], T[:, 0:m, :]
                d0 = ps[2][0:P, 0:m * D].rearrange("p (c f) -> p c f", f=D)
                d1 = ps[3][0:P, 0:m * D].rearrange("p (c f) -> p c f", f=D)
                bb = BB.rearrange("p (a f) -> p a f", a=1).broadcast_to([P, m, D])

                def own(v, j):
                    return v[:, c0 + j:c0 + j + 1]

                if not kind.startswith("gru"):
                    if b >= 2:
                        wait("tf_done", plan.get(("tf_done", s, b - 2)))
                        for i in (f"x2_stored{b % 2}", f"out_stored{b % 2}"):
                            wait(i, plan.get((i, s, b - 2)))
                    else:
                        wait("tf_done", before("tf_done", s, 0))
                if kind == "prep":
                    wait("x_in", 16)
                    each(m, lambda j: dve.tensor_scalar(u[:, j, :], XALL[:, c0 + j, :], own(dinv, j), None, ALU.mult), "u_ready")
                    split2(u, cs, pout, sc[0:P, 0:1])
                    return
                wait("stage_w", val("stage_w", s))
                if not kind.startswith("gru"):
                    wait("dense_done", val("dense_done", s, b))
                if kind in ("gcn0", "gcn1"):
                    each(m, lambda j: dve.scalar_tensor_tensor(u[:, j, :], d0[:, j, :], own(dinv, j), BB,
                                                               ALU.mult, ALU.add), "dense_free")
                if kind == "gcn0":
                    step(dve.tensor_scalar(t, u, 0.0, ab[:, 0:1], ALU.min, ALU.mult))
                    step(dve.scalar_tensor_tensor(u, u, 0.0, t, ALU.max, ALU.add))
                    wait("rx_in", val("rx_in", s, b))
                    step(dve.tensor_tensor(u, u, RX[:, 0:m, :], ALU.add), "rx_free")
                    norm(s, b, u, m, "u_ready")
                    split2(u, cs, pout)
                if kind in ("sage1", "sage2"):
                    step(dve.tensor_tensor(u, d1, bb, ALU.add))
                    each(m, lambda j: dve.scalar_tensor_tensor(u[:, j, :], d0[:, j, :], own(s1, j), u[:, j, :],
                                                               ALU.mult, ALU.add), "dense_free")
                if kind == "sage1":
                    step(dve.tensor_scalar(u, u, 0.0, None, ALU.max), "u_ready")
                    split2(u, cs, pout, sc[0:P, 1:2])
                if kind == "sage2":
                    step(dve.tensor_tensor(t, PB[0][:, cs, :], PB[1][:, cs, :], ALU.add))
                    step(dve.scalar_tensor_tensor(u, t, 1.0 / SCALE, u, ALU.mult, ALU.add))
                    norm(s, b, u, m, "u_ready")
                    split2(u, cs, pout)
                if kind == "gcn1":
                    step(dve.scalar_tensor_tensor(u, u, 0.2, u, ALU.mult, ALU.max))
                    each(m, lambda j: dve.tensor_scalar(u[:, j, :], u[:, j, :], own(dinv, j), None, ALU.mult), "u_ready")
                    split2(u, cs, pout, sc[0:P, 2:3])
                if kind == "gcn2":
                    each(m, lambda j: dve.scalar_tensor_tensor(u[:, j, :], d0[:, j, :], own(dinv, j), WB[0:P],
                                                               ALU.mult, ALU.mult), "dense_free")
                    step(dve.tensor_tensor(u, u, bb, ALU.add))
                    step(dve.tensor_tensor(t, PB[0][:, cs, :], PB[1][:, cs, :], ALU.add))
                    step(dve.tensor_scalar(t, t, 1.0 / SCALE, None, ALU.mult))
                    each(m, lambda j: dve.scalar_tensor_tensor(u[:, j, :], t[:, j, :], own(sd, j), u[:, j, :],
                                                               ALU.mult, ALU.add))
                    norm(s, b, u, m, "u_ready")
                if kind.startswith("gru"):
                    o_, q = cols(b)
                    r, z, g_, nx = GR[:, 0:q], GZ[:, 0:q], GT[:, 0:q], NX[:, 0:q]
                    wait("r_ready", val("r_ready", s, b))
                    step(dve.scalar_tensor_tensor(r, ps[5][:, 0:q], gb[:, 5:6], r, ALU.add, ALU.mult))
                    wait("z_ready", val("z_ready", s, b))
                    step(dve.tensor_tensor(r, r, ps[4][:, 0:q], ALU.add), "pre_n")
                    wait("n_ready", val("n_ready", s, b))
                    step(dve.tensor_tensor(g_, XT[:, o_:o_ + q], r, ALU.subtract))
                    step(dve.tensor_tensor(g_, g_, z, ALU.mult))
                    wait("tn_done", before("tn_done", s, b))
                    wait("nx_copied", before("nx_copied", s, b))
                    step(dve.tensor_tensor(nx, r, g_, ALU.add), "nx_ready")
                    wait("tn_done", val("tn_done", s, b))
                    tn = ps[6][0:P, 0:m * D].rearrange("p (c f) -> p c f", f=D)
                    if kind == "gru":
                        split2(tn, cs, pout)
                    else:
                        wait("rx_in", val("rx_in", s, b))
                        y = Y[:, 0:m, :]
                        step(dve.scalar_tensor_tensor(y, y, 2.0, tn, ALU.mult, ALU.add), "tn_free")
                        norm(s, b, y, m)
                        each(m, lambda j: dve.tensor_scalar(y[:, j, :], y[:, j, :], own(dinv, j), None, ALU.mult), "u_ready")
                        split2(y, cs, pout)

            for s in range(NS):
                if STAGES[s][0] == "prep":
                    for b in range(NB):
                        elem(s, b)
                    continue
                evac(s, 0)
                for b in range(NB):
                    if b + 1 < NB:
                        evac(s, b + 1)
                    elem(s, b)

        @block.tensor
        def _(pe):
            pe.wait_ge(S["weights_in"], 16 * 18)
            pe.wait_ge(S["consts"], CONST_EARLY)
            for g in range(4):
                for k in range(4 * g, min(4 * g + 4, 14)):
                    i = pe.transpose(ps[g][:, (k % 4) * D:(k % 4 + 1) * D], WR[:, k * D:(k + 1) * D], ident)
                i.then_inc(S["weights_turned"], 1)
            pe.matmul(ps[7][0:1, 0:D], ctxc, WGB[:, 0:D], start=True, stop=True)
            pe.matmul(ps[7][0:1, D:2 * D], ctxc, WGB[:, D:2 * D], start=True, stop=True).then_inc(S["rows_mm"], 1)
            pe.wait_ge(S["turned_kept"], 4)
            for l in range(4):
                pe.matmul(ps[l][:, 0:3 * D], TW[:, (10 + l) * D:(11 + l) * D], TW[:, 4 * D:7 * D],
                          start=True, stop=True).then_inc(S["wc_mm"], 1)
            for g in range(4):
                if g == 0:
                    pe.wait_ge(S["dve_step"], step_at["keyd"])
                else:
                    pe.wait_ge(S["keys_kept"], g)
                what = dw if g < 2 else es
                for j in range(4):
                    jj = 4 * (g % 2) + j
                    i = pe.transpose(ps[6][0:P, j * EP:(j + 1) * EP], what[:, jj * P:(jj + 1) * P], ident[0:EP, 0:EP])
                i.then_inc(S["keys_turned"], 1)

            pe.wait_ge(S["tab_back"], 16)
            pe.wait_ge(S["wc_done"], 4)
            done = pe.alloc_register("pe_steps_done")
            pe.reg_mov(done, 0)
            pe.sem_inc(S["hot_free"], 2)
            regs = [pe.alloc_register(f"pe_{what}{q}") for q in range(WQ) for what in ("first", "count")]

            def window(w, q, bank):
                count = pe.snap(regs[2 * q + 1], min_val=1, max_val=EC // K)
                pe.wait_ge(S["win_kept"], w + 1)
                pe.matmul(ps[bank][:, 0:2], ZZ, ZZ[:, 0:2], start=True, stop=False, skip_group_check=True)
                with pe.Fori(0, count) as _i:
                    t = pe.snap(done, min_val=0, max_val=1 << 20)
                    for h in range(2):
                        pe.wait_ge(S["hot_ready"], t * 4 + (4 * RR + 2 * h + 2))
                        for k in range(KH):
                            i = pe.matmul(ps[bank][:, 0:WC], LR[:, h, :, k], MR[:, h, :, k], start=False, stop=False,
                                          skip_group_check=True)
                        i.then_inc(S["hot_free"], 1)
                    pe.reg_add(done, done, 1)
                pe.matmul(ps[bank][:, 0:2], ZZ, ZZ[:, 0:2], start=False, stop=True,
                          skip_group_check=True).then_inc(S["win_done"], 1)

            with pe.Fori(0, NWIN // WQ) as quad:
                pe.load(regs, TAB[0:1, bass.ds(quad * (2 * WQ), 2 * WQ)])
                for q in range(WQ):
                    window(quad * WQ + q, q, q % 2)

            pe.wait_ge(S["deg_in"], 16)
            for c in range(NC):
                i = pe.matmul(ps[7][0:P, c:c + 1], DEGR[:, c * P:(c + 1) * P], ones[0:NC, 0:1], start=True, stop=True)
            i.then_inc(S["deg_mm"], 1)

            def wait(name, v):
                if v:
                    pe.wait_ge(S[name], v)

            def spmm(s, b):
                pin = STAGES[s][1]
                o_, m = cols(b)
                g = val("agg_done", s, b)
                if g > 2:
                    wait("ag_ready", g - 2)
                agg = ps[g % 2][:, 0:m]
                for k in range(NC):
                    if b == 0 and k % CPB == 0:
                        if k // CPB >= NB - 2 or s == 1:
                            turn(s - 1, k // CPB)
                        wait("parts_done", val("parts_done", s - 1, k // CPB))
                    for q, part in enumerate(pin):
                        i = pe.matmul(agg, part[:, k, :], AT[:, k, o_:o_ + m], start=k == 0 and q == 0,
                                      stop=k == NC - 1 and q == len(pin) - 1)
                i.then_inc(S["agg_done"], 1)

            def dense(s, b):
                kind = STAGES[s][0]
                o_, m = cols(b)
                if b == 0:
                    wait("stage_w", val("stage_w", s))
                wait("ag_ready", val("ag_ready", s, b))
                wait("dense_free", before("dense_free", s, b))
                wait("pre_n", before("pre_n", s, b))
                if kind.startswith("gru"):
                    xt = XT[:, o_:o_ + m]
                    if STAGES[s - 1][0] == "gru":
                        wait("nx_copied", val("nx_copied", s - 1, b))
                    else:
                        wait("xt_ready", val("xt_ready", s - 1, b))
                    for g in range(2):
                        pe.matmul(ps[2 + g][:, 0:m], WCG[:, g * D:(g + 1) * D], AG[:, 0:m], start=True, stop=False)
                        pe.matmul(ps[2 + g][:, 0:m], WHH[:, g * D:(g + 1) * D], xt, start=False, stop=True)
                    pe.matmul(ps[4][:, 0:m], WCG[:, 2 * D:3 * D], AG[:, 0:m], start=True, stop=True)
                    i = pe.matmul(ps[5][:, 0:m], WHH[:, 2 * D:3 * D], xt, start=True, stop=True)
                else:
                    if kind.startswith("sage"):
                        wait("xs_ready", val("xs_ready", s, b))
                    for j in range(chunks_of(b)):
                        i = pe.matmul(ps[2][0:P, j * D:(j + 1) * D], AG[:, j * P:(j + 1) * P], WA, start=True, stop=True)
                        if kind.startswith("sage"):
                            i = pe.matmul(ps[3][0:P, j * D:(j + 1) * D], XS[:, j * P:(j + 1) * P], WB, start=True, stop=True)
                i.then_inc(S["dense_done"], 1)

            def turn(s, b):
                kind = STAGES[s][0]
                if kind.startswith("gru"):
                    wait("nx_ready", val("nx_ready", s, b))
                    prev = (s, b - 1) if b else (s - 1, NB - 1)
                    if STAGES[prev[0]][0] == "gru":
                        wait("parts_done", val("parts_done", *prev))
                    elif b:
                        wait("tn_free", val("tn_free", *prev))
                    for j in range(chunks_of(b)):
                        i = pe.transpose(ps[6][0:P, j * D:(j + 1) * D], NX[:, j * P:(j + 1) * P], ident)
                    i.then_inc(S["tn_done"], 1)
                if ("u_ready", s, b) in plan and kind != "gcn2":
                    wait("u_ready", val("u_ready", s, b))
                    wait("xt_ready", before("xt_ready", s, b))
                    v = Y if kind == "gru_last" else U2[b % 2]
                    for j in range(chunks_of(b)):
                        i = pe.transpose(ps[7][:, j * P:(j + 1) * P], v[:, j, :], ident[0:P, 0:P])
                    i.then_inc(S["tf_done"], 1)

            for s in range(1, NS):
                spmm(s, 0)
                for b in range(NB):
                    if b + 1 < NB:
                        spmm(s, b + 1)
                    dense(s, b)
                    if 0 < b < NB - 1:
                        turn(s, b - 1)

        @block.scalar
        def _(act):
            for g in range(4):
                act.wait_ge(S["weights_turned"], g + 1)
                m = (4 if g < 3 else 2) * D
                act.activation(TW[:, 4 * g * D:4 * g * D + m], ps[g][:, 0:m], ACT.Copy).then_inc(S["turned_kept"], 1)
            for l in range(4):
                act.wait_ge(S["wc_mm"], l + 1)
                act.activation(WCT[:, 3 * D * l:3 * D * (l + 1)], ps[l][:, 0:3 * D], ACT.Copy).then_inc(S["wc_done"], 1)
            act.wait_ge(S["gate_pre"], 1)
            act.activation(row[:, 2 * D:3 * D], row[:, 2 * D:3 * D], ACT.Sigmoid).then_inc(S["gate_done"], 1)

            act.sem_inc(S["win_kept"], 2)

            def keep(w, bank, m):
                act.wait_ge(S["win_done"], w + 1)
                v = ps[bank][0:P + 1, 0:WC].rearrange("p (c d) -> p c d", d=W)[:, :, 0:m]
                act.activation(ATX[:, :, bass.ds(w * W, m)], v, ACT.Copy, scale=HALF).then_inc(S["win_kept"], 1)

            with act.Fori(0, NWIN // 2 - 1) as pair:
                keep(pair * 2, 0, W)
                keep(pair * 2 + 1, 1, W)
            keep(NWIN - 2, 0, W)
            keep(NWIN - 1, 1, LASTW)

            act.wait_ge(S["deg_plus"], 1)
            act.activation(sd, sd, ACT.Sqrt).then_inc(S["deg_root"], 1)
            act.wait_ge(S["sums_done"], 1)
            act.activation(sq, sq, ACT.Sqrt).then_inc(S["bounds_root"], 1)

            def wait(name, v):
                if v:
                    act.wait_ge(S[name], v)

            def evac(s, b):
                kind = STAGES[s][0]
                if kind not in ("sage1", "sage2", "gru", "gru_last"):
                    return
                o_, m = cols(b)
                wait("dense_done", before("dense_done", s, b))
                if kind.startswith("sage"):
                    if b == 0:
                        wait("rx_free", total["rx_free"])
                    wait("xt_ready", val("xt_ready", s - 1, b))
                    act.activation(XS[:, 0:m], XT[:, o_:o_ + m], ACT.Copy).then_inc(S["xs_ready"], 1)
                wait("agg_done", val("agg_done", s, b))
                agg = ps[val("agg_done", s, b) % 2][:, 0:m]
                scale = si[:, 1:2] if kind == "sage2" else 1.0 / (SCALE * HALF)
                wait("scales_ready", 1)
                act.activation(AG[:, 0:m], agg, ACT.Copy, scale=scale).then_inc(S["ag_ready"], 1)

            def keep_turned(s, b):
                if ("xt_ready", s, b) in plan:
                    o_, m = cols(b)
                    wait("tf_done", val("tf_done", s, b))
                    act.activation(XT[:, o_:o_ + m], ps[7][:, 0:m], ACT.Copy).then_inc(S["xt_ready"], 1)

            def gates(s, b):
                kind = STAGES[s][0]
                o_, q = cols(b)
                m = chunks_of(b)
                if kind.startswith("gru"):
                    wait("dense_done", val("dense_done", s, b))
                    wait("x2_stored0", total["x2_stored0"])
                    wait("x2_stored1", total["x2_stored1"])
                    wait("tf_done", before("tf_done", 4, 0))
                    wait("parts_done", before("parts_done", 4, 0))
                    wait("nx_ready", before("nx_ready", s, b))
                    act.activation(GR[:, 0:q], ps[2][:, 0:q], ACT.Sigmoid, bias=gb[:, 0:1]).then_inc(S["r_ready"], 1)
                    act.activation(GZ[:, 0:q], ps[3][:, 0:q], ACT.Sigmoid, bias=gb[:, 1:2]).then_inc(S["z_ready"], 1)
                    wait("pre_n", val("pre_n", s, b))
                    act.activation(GR[:, 0:q], GR[:, 0:q], ACT.Tanh, bias=gb[:, 2:3]).then_inc(S["n_ready"], 1)
                if kind == "gru":
                    wait("nx_ready", val("nx_ready", s, b))
                    act.activation(XT[:, o_:o_ + q], NX[:, 0:q], ACT.Copy).then_inc(S["nx_copied"], 1)
                if kind in ("gcn0", "sage2", "gru_last", "gcn2"):
                    wait("var_ready", val("var_ready", s, b))
                    act.activation(rs[:, 0:m], rs[:, 0:m], ACT.Sqrt).then_inc(S["sd_ready"], 1)

            for b in range(NB):
                keep_turned(0, b)
            for s in range(1, NS):
                evac(s, 0)
                for b in range(NB):
                    if b + 1 < NB:
                        evac(s, b + 1)
                    if 0 < b < NB - 1:
                        keep_turned(s, b - 1)
                    gates(s, b)
                keep_turned(s, NB - 2)
                keep_turned(s, NB - 1)


_INS = ['x', 'src', 'dst', 'L0_gnn_W', 'L0_gnn_b', 'L0_gnn_a', 'L1_gnn_W1_l', 'L1_gnn_b1', 'L1_gnn_W1_r',
        'L1_gnn_W2_l', 'L1_gnn_b2', 'L1_gnn_W2_r', 'L2_gnn_weight', 'L2_gnn_w_ih', 'L2_gnn_w_hh', 'L2_gnn_b_ih',
        'L2_gnn_b_hh', 'L3_gnn_ctx', 'L3_gnn_W1', 'L3_gnn_b1', 'L3_gnn_W2', 'L3_gnn_b2', 'L3_gnn_Wg', 'L3_gnn_bg',
        'L3_gnn_Wb']

_OUT = ((N, D), "float32")


def kernel(**inputs):
    import numpy as np
    import concourse.bacc as bacc
    from concourse.bass_utils import run_bass_kernel_spmd

    nc = bacc.Bacc("TRN2", target_bir_lowering=False, num_devices=1)
    arrays, args = {}, []
    for name in _INS:
        a = np.ascontiguousarray(inputs[name])
        if a.ndim == 0:
            a = a.reshape(1)
        arrays[f"in_{name}"] = a
        args.append(nc.dram_tensor(f"in_{name}", a.shape, mybir.dt.from_np(a.dtype), kind="ExternalInput").ap())
    out = nc.dram_tensor("out", _OUT[0], mybir.dt.from_np(np.dtype(_OUT[1])), kind="ExternalOutput").ap()
    build(nc, *args, out)
    r = run_bass_kernel_spmd(nc, [arrays], core_ids=[0])
    return r.results[0]["out"]
```

```python
from contextlib import ExitStack

import concourse.bass as bass
from concourse import mybir

F32 = mybir.dt.float32
F16 = mybir.dt.float16
I32 = mybir.dt.int32
ALU = mybir.AluOpType
ACT = mybir.ActivationFunctionType
AX = mybir.AxisListType

D = 128
P = 125
N = 3125
NC = N // P
E = 100000
EC = E // P
W = 16
WC = NC * W
NWIN = -(-N // W)
LASTW = N - (NWIN - 1) * W
K = 4
KH = K // 2
RR = 2
ECP = EC + K
WP = NWIN // 2
WQ = 14
EP, EJ = 100, 8
BIG = 1024.0
HALF = 0.5
ROUND = 12582912.0
BLOCKS = (4, 4, 4, 4, 3, 3, 3)
START = [sum(BLOCKS[:b]) for b in range(len(BLOCKS))]
NB, CPB = len(BLOCKS), max(BLOCKS)
assert sum(BLOCKS) == NC and NWIN % WQ == 0 and WQ % 2 == 0
SCALE = 4096.0
ROWB = 11.5
EPS = 1e-5




def chunks_of(b):
    return BLOCKS[b]


def build(nc, x_d, src_d, dst_d, w0_d, b0_d, a_d, w1l_d, b1_d, w1r_d, w2l_d, b2_d, w2r_d,
          gw_d, wih_d, whh_d, bih_d, bhh_d, ctx_d, w31_d, b31_d, w32_d, b32_d, wg_d, bg_d, wb_d, out_d):
    cm_s = nc.dram_tensor("chunk_bounds", [2, EC], F32, kind="Internal").ap()
    tab_s = nc.dram_tensor("window_table", [WP * 4], I32, kind="Internal").ap()
    wt_s = nc.dram_tensor("weights_turned", [4, D, D], F32, kind="Internal").ap()
    whh_s = nc.dram_tensor("whh_turned", [D, 3 * D], F32, kind="Internal").ap()
    wc_s = nc.dram_tensor("gate_weights", [4, D, 3 * D], F32, kind="Internal").ap()
    rows_s = nc.dram_tensor("gate_rows", [2, D], F32, kind="Internal").ap()
    x2_s = nc.dram_tensor("x2", [N, D], F32, kind="Internal").ap()

    with ExitStack() as ctx:
        def sem(name):
            return ctx.enter_context(nc.semaphore(name))

        counts = ctx.enter_context(nc.sbuf_tensor("counts", [128, NC * N + 1], F16))
        ATX = counts[0:P + 1, 0:NC * N].rearrange("p (c d) -> p c d", c=NC)
        AT = ATX[0:P]
        before_counts = counts.bitcast(F32)

        def pre(off, count, parts=128):
            return before_counts[0:parts, off:off + count]

        ARENA = 56576
        arena = ctx.enter_context(nc.sbuf_tensor("arena", [128, ARENA // 4], F32))

        def at(off, count, dt=F32, parts=128):
            size = 2 if dt == F16 else 4
            assert off % 4 == 0 and off + count * size <= ARENA, (off, count)
            words = -(-count * size // 4)
            v = arena[0:parts, off // 4:off // 4 + words]
            return (v if dt == F32 else v.bitcast(dt))[:, 0:count]

        O_XT, O_PA, O_PB, O_AG = 0, 12512, 31712, 44512
        O_XS, O_U, O_W = 46528, 48576, 50624
        O_ID, O_SM = 54208, 54720
        XT = at(O_XT, N)
        PA = [at(O_PA + 6400 * k, NC * D, F16, P).rearrange("p (c f) -> p c f", f=D) for k in range(2)]
        PB = [at(O_PB + 6400 * k, NC * D, F16, P).rearrange("p (c f) -> p c f", f=D) for k in range(2)]
        AG = at(O_AG, CPB * P)
        XS = at(O_XS, CPB * P)
        RX = at(O_XS, CPB * D, F32, P).rearrange("p (c f) -> p c f", f=D)
        U2 = [at(o, CPB * D, F32, P).rearrange("p (c f) -> p c f", f=D) for o in (O_U, O_PA + 12800)]
        XALL = at(O_PB, NC * D, F32, P).rearrange("p (c f) -> p c f", f=D)
        WA = at(O_W, D)
        WB = at(O_W + 512, D)
        BB = at(O_W + 1024, D, F32, P)
        T = at(O_W + 1536, CPB * D, F32, P).rearrange("p (c f) -> p c f", f=D)
        WCG = at(O_W, 3 * D)
        WHH = at(O_W + 1536, 3 * D)
        O_P3 = O_PA + 12800
        GR = at(O_XS, CPB * P)
        GZ = at(O_U, CPB * P)
        NX = at(O_P3 + 2048, CPB * P)
        X3 = at(O_P3, CPB * D, F32, P).rearrange("p (c f) -> p c f", f=D)
        X2 = at(O_P3 + 4096, CPB * D, F32, P).rearrange("p (c f) -> p c f", f=D)
        ident = at(O_ID, D)
        o = O_SM
        small = {}
        for name, cnt in (("dinv", NC), ("s1", NC), ("sd", NC), ("mv", 2 * CPB), ("rs", CPB), ("ab", 1),
                          ("gb", 6), ("st", 6 * CPB), ("sq", 3), ("mx", 3), ("sc", 3), ("si", 3), ("bd", 3), ("bc", 2)):
            small[name] = at(o, cnt)
            o += cnt * 4
        dinv, s1, sd = (small[k][0:P] for k in ("dinv", "s1", "sd"))
        mv = small["mv"][0:P].rearrange("p (c t) -> p c t", t=2)
        st = small["st"][0:P].rearrange("p (c t) -> p c t", t=6)
        rs, ab = small["rs"][0:P], small["ab"][0:P]
        gb = small["gb"]
        sq, mx, sc, si, bd, bc = (small[k] for k in ("sq", "mx", "sc", "si", "bd", "bc"))
        ones = at(o, 2, F16, P)
        W31R = at(42496, D)
        SQT = at(43520, D)
        DEGR = at(0, N, F16, NC)

        iotax = at(0, WC * KH, F16, P).rearrange("p (n k) -> p n k", k=KH)
        KL = at(4000, 2 * ECP, F32, P).rearrange("p (t c) -> p t c", t=2)
        MR = at(10880, K * WC, F16, P).rearrange("p (h n k) -> p h n k", h=2, k=KH)
        LR = at(23680, K * 128, F16, P).rearrange("p (h n k) -> p h n k", h=2, k=KH)
        KR = at(27776, RR * 2 * K, F16, P)
        TOT = at(25728, 1, I32, 1)
        TOTF = at(25732, 1, F32, 1)
        CNTF = at(25736, NWIN, F32, 1)
        WT = at(27840, 2 * NWIN, F32, P).rearrange("p (t c) -> p t c", t=2)
        ZZ = at(29408, 128, F16, P)
        TAB = at(29664, WP * 4, I32, 1)
        ei = at(10880, EJ * P, I32, EP)
        ef = at(14880, EJ * P, F32, EP)
        eh = at(18880, EJ * P, F32, EP)
        es = at(22880, EJ * P, F32, EP)
        di = at(30400, EJ * P, I32, EP)
        df = at(34400, EJ * P, F32, EP)
        dw = at(38400, EJ * P, F32, EP)
        CM = at(42400, 2 * EJ, F32, EP)
        CB = at(30400, 2 * EC, F32, WP)
        CI = at(36800, EC, F32, WP)
        TMP = at(40000, EC, F32, WP)
        WID = at(43200, 2, F32, WP)
        WM = at(43208, 8, F32, WP)
        TBI = at(43240, 4, I32, WP)
        WR = at(O_AG, 14 * D)
        TW = pre(0, 14 * D)
        WCT = pre(14 * D, 12 * D)
        WGB = pre(26 * D, 2 * D, 64)
        XE = pre(28 * D, NC * D, P)
        CF = pre(28 * D + NC * D, EC, WP)
        row = at(51680, 4 * D, F32, 1)
        ctxc = at(53728, 1, F32, 64)

        ps = [ctx.enter_context(nc.psum_tensor(f"bank{i}", [128, 512], F32)) for i in range(8)]

        names = (
            "edges_in sources_in weights_in x_early x_in deg_in cm_stored cm_back tab_stored tab_back wc_kept "
            "rows_kept "
            "consts weights_turned turned_kept wc_mm wc_done rows_mm gate_pre gate_done rows_done "
            "sums_ready sums_done max_ready max_done bounds_root scales_ready "
            "dve_step keys_turned keys_kept key_rel keys_made hot_ready hot_made hot_free win_done win_kept "
            "deg_mm deg_plus deg_root "
            "stage_w rx_in rx_free parts_done agg_done ag_ready dense_done dense_free xs_ready xt_ready u_ready "
            "tn_done tn_free tf_done "
            "sd_ready var_ready r_ready z_ready pre_n n_ready nx_ready nx_copied x2_stored0 x2_stored1 "
            "out_stored0 out_stored1 "
        ).split()
        S = {n: sem(n) for n in names}
        block = ctx.enter_context(nc.Block())

        STAGES = [("prep", None, PA), ("gcn0", PA, PB), ("sage1", PB, PA), ("sage2", PA, PB),
                  ("gru", PB, PA), ("gru", PA, PB), ("gru", PB, PA),
                  ("gru_last", PA, PB), ("gcn1", PB, PA), ("gcn2", PA, None)]
        NS = len(STAGES)
        gru_no = {4: 0, 5: 1, 6: 2, 7: 3}

        def cols(b):
            return P * START[b], P * chunks_of(b)

        plan = {}
        total = {}

        def event(name, key, inc=1):
            total[name] = total.get(name, 0) + inc
            plan[(name,) + key] = total[name]

        for s, (kind, pin, pout) in enumerate(STAGES):
            if kind != "prep":
                loads = {"gcn0": 2, "sage1": 3, "sage2": 3, "gru": 2, "gru_last": 2, "gcn1": 2, "gcn2": 3}[kind]
                event("stage_w", (s,), 16 * loads)
            for b in range(NB):
                k = (s, b)
                own = []
                if kind in ("gcn0", "gru_last"):
                    event("rx_in", k, 16)
                if kind == "gcn0":
                    own += ["rx_free"]
                if kind != "prep":
                    own += ["agg_done", "ag_ready", "dense_done"]
                if kind in ("gcn0", "sage1", "sage2", "gcn1", "gcn2"):
                    own += ["dense_free", "u_ready"]
                if kind in ("prep", "gru_last"):
                    own += ["u_ready"]
                if kind.startswith("sage"):
                    own += ["xs_ready"]
                if kind not in ("gru", "gcn2"):
                    own += ["tf_done", "xt_ready"]
                if kind.startswith("gru"):
                    own += ["r_ready", "z_ready", "pre_n", "n_ready", "nx_ready", "tn_done"]
                if kind == "gru":
                    own += ["nx_copied"]
                if kind == "gru_last":
                    own += ["tn_free"]
                if kind in ("gcn0", "sage2", "gru_last", "gcn2"):
                    own += ["var_ready", "sd_ready"]
                if pout is not None:
                    own += ["parts_done"]
                for n in own:
                    event(n, k)
                if kind == "sage2":
                    event(f"x2_stored{b % 2}", k, 16)
                if kind == "gcn2":
                    event(f"out_stored{b % 2}", k, 16)

        def val(name, s, b=None):
            return plan[(name, s) if b is None else (name, s, b)]

        def before(name, s, b):
            keys = [(name, t, c) for t in range(s + 1) for c in range(NB) if (t, c) < (s, b)]
            for k in reversed(keys):
                if k in plan:
                    return plan[k]
            return None

        step_at = {"bounds": 7, "keyd": 13, "table": 33}

        @block.sync
        def _(sp):
            sp.dma_start(di, dst_d.rearrange("(p f) -> p f", p=EP)).then_inc(S["edges_in"], 16)
            sp.dma_start(ei, src_d.rearrange("(p f) -> p f", p=EP)).then_inc(S["sources_in"], 16)
            for k, w in enumerate((w1l_d, w1r_d, w2l_d, w2r_d)):
                sp.dma_start(WR[:, k * D:(k + 1) * D], w).then_inc(S["weights_in"], 16)
            sp.dma_start(WR[:, 4 * D:7 * D].rearrange("p (g i) -> p g i", g=3),
                         wih_d.rearrange("(g p) i -> p g i", p=D)).then_inc(S["weights_in"], 16)
            sp.dma_start(WR[:, 7 * D:10 * D].rearrange("p (g i) -> p g i", g=3),
                         whh_d.rearrange("(g p) i -> p g i", p=D)).then_inc(S["weights_in"], 16)
            sp.dma_start(WR[:, 10 * D:14 * D].rearrange("p (l i) -> p l i", l=4),
                         gw_d.rearrange("l p i -> p l i")).then_inc(S["weights_in"], 16)
            sp.dma_start(WGB[:, 0:D], wg_d).then_inc(S["weights_in"], 16)
            sp.dma_start(WGB[:, D:2 * D], wb_d).then_inc(S["weights_in"], 16)
            sp.dma_start(ctxc, ctx_d.rearrange("a k -> k a")).then_inc(S["weights_in"], 16)
            sp.dma_start(W31R, w31_d).then_inc(S["weights_in"], 16)
            sp.dma_start(bc[:, 0:1], b1_d.rearrange("(p a) -> p a", a=1)).then_inc(S["weights_in"], 16)
            sp.dma_start(bc[:, 1:2], b31_d.rearrange("(p a) -> p a", a=1)).then_inc(S["weights_in"], 16)
            sp.dma_start(row[:, 0:D], bg_d.rearrange("(a k) -> a k", a=1)).then_inc(S["weights_in"], 16)
            sp.dma_start(row[:, D:2 * D], b32_d.rearrange("(a k) -> a k", a=1)).then_inc(S["weights_in"], 16)
            sp.dma_start(gb[:, 0:3], bih_d.rearrange("(g p) -> p g", p=D),
                         allow_slow_non_contiguous=True).then_inc(S["weights_in"], 16)
            sp.dma_start(gb[:, 3:6], bhh_d.rearrange("(g p) -> p g", p=D),
                         allow_slow_non_contiguous=True).then_inc(S["weights_in"], 16)
            sp.dma_start(ab, a_d.rearrange("(a b) -> a b", a=1).to_broadcast([P, 1])).then_inc(S["weights_in"], 16)
            sp.dma_start(XE.rearrange("p (c f) -> p c f", f=D),
                         x_d.rearrange("(c p) f -> p c f", p=P)).then_inc(S["x_early"], 16)
            sp.wait_ge(S["dve_step"], step_at["bounds"])
            sp.dma_start(cm_s.rearrange("t (p j) -> p t j", p=EP),
                         CM.rearrange("p (t j) -> p t j", t=2)).then_inc(S["cm_stored"], 16)
            sp.wait_ge(S["cm_stored"], 16)
            for t in range(2):
                sp.dma_start(CB[:, t * EC:(t + 1) * EC],
                             cm_s[t:t + 1, :].to_broadcast([WP, EC])).then_inc(S["cm_back"], 16)
            sp.wait_ge(S["turned_kept"], 4)
            sp.dma_start(wt_s.rearrange("k p i -> p k i"),
                         TW[:, 0:4 * D].rearrange("p (k i) -> p k i", k=4)).then_inc(S["wc_kept"], 16)
            sp.dma_start(whh_s, TW[:, 7 * D:10 * D]).then_inc(S["wc_kept"], 16)
            sp.wait_ge(S["wc_done"], 4)
            sp.dma_start(wc_s.rearrange("l p i -> p l i"),
                         WCT.rearrange("p (l i) -> p l i", l=4)).then_inc(S["wc_kept"], 16)
            sp.wait_ge(S["rows_done"], 1)
            sp.dma_start(rows_s, row[:, 2 * D:4 * D]).then_inc(S["rows_kept"], 16)
            sp.wait_ge(S["dve_step"], step_at["table"])
            sp.dma_start(tab_s.rearrange("(p k) -> p k", p=WP), TBI).then_inc(S["tab_stored"], 16)
            sp.wait_ge(S["tab_stored"], 16)
            sp.dma_start(TAB, tab_s.rearrange("(a k) -> a k", a=1)).then_inc(S["tab_back"], 16)
            sp.dma_start(XALL, x_d.rearrange("(c p) f -> p c f", p=P)).then_inc(S["x_in"], 16)
            sp.wait_ge(S["rows_kept"], 16)
            sp.wait_ge(S["win_kept"], 2 + NWIN)
            sp.wait_ge(S["hot_made"], 1)
            sp.wait_ge(S["keys_made"], 1)
            sp.dma_start(DEGR, counts[P:P + 1, 0:NC * N]).then_inc(S["deg_in"], 16)

            xv = x_d.rearrange("(c p) f -> p c f", p=P)
            x2v = x2_s.rearrange("(c p) f -> p c f", p=P)
            ov = out_d.rearrange("(c p) f -> p c f", p=P)
            for s, (kind, pin, pout) in enumerate(STAGES):
                if kind != "prep":
                    v = before("dense_done", s, 0)
                    if v:
                        sp.wait_ge(S["dense_done"], v)
                    v = before("parts_done", s, 0)
                    if v:
                        sp.wait_ge(S["parts_done"], v)
                q = S["stage_w"]
                if kind == "gcn0":
                    sp.dma_start(WA, w0_d).then_inc(q, 16)
                    sp.dma_start(BB, b0_d.rearrange("(a k) -> a k", a=1).to_broadcast([P, D])).then_inc(q, 16)
                if kind in ("sage1", "sage2"):
                    k = 0 if kind == "sage1" else 2
                    sp.dma_start(WA, wt_s[k]).then_inc(q, 16)
                    sp.dma_start(WB, wt_s[k + 1]).then_inc(q, 16)
                    bias = b1_d if kind == "sage1" else b2_d
                    sp.dma_start(BB, bias.rearrange("(a k) -> a k", a=1).to_broadcast([P, D])).then_inc(q, 16)
                if kind.startswith("gru"):
                    sp.dma_start(WCG, wc_s[gru_no[s]]).then_inc(q, 16)
                    sp.dma_start(WHH, whh_s).then_inc(q, 16)
                if kind == "gcn1":
                    sp.dma_start(WA, w31_d).then_inc(q, 16)
                    sp.dma_start(BB, b31_d.rearrange("(a k) -> a k", a=1).to_broadcast([P, D])).then_inc(q, 16)
                if kind == "gcn2":
                    sp.dma_start(WA, w32_d).then_inc(q, 16)
                    sp.dma_start(WB[0:P], rows_s[0:1, :].to_broadcast([P, D])).then_inc(q, 16)
                    sp.dma_start(BB, rows_s[1:2, :].to_broadcast([P, D])).then_inc(q, 16)
                for b in range(NB):
                    n = chunks_of(b)
                    cs = slice(START[b], START[b] + n)
                    if kind in ("gcn0", "gru_last"):
                        if kind == "gcn0" and b:
                            sp.wait_ge(S["rx_free"], val("rx_free", s, b - 1))
                        if kind == "gru_last" and b:
                            sp.wait_ge(S["tn_free"], val("tn_free", s, b - 1))
                        if kind == "gru_last" and b == 0:
                            for i in ("x2_stored0", "x2_stored1"):
                                sp.wait_ge(S[i], total[i])
                        to = X2 if kind == "gru_last" else RX
                        frm = x2v if kind == "gru_last" else xv
                        sp.dma_start(to[:, 0:n, :], frm[:, cs, :]).then_inc(S["rx_in"], 16)
                    if kind == "sage2":
                        sp.wait_ge(S["u_ready"], val("u_ready", s, b))
                        sp.dma_start(x2v[:, cs, :], U2[b % 2][:, 0:n, :]).then_inc(S[f"x2_stored{b % 2}"], 16)
                    if kind == "gcn2":
                        sp.wait_ge(S["u_ready"], val("u_ready", s, b))
                        sp.dma_start(ov[:, cs, :], U2[b % 2][:, 0:n, :]).then_inc(S[f"out_stored{b % 2}"], 16)
            for i in ("out_stored0", "out_stored1"):
                sp.wait_ge(S[i], total[i])

        @block.gpsimd
        def _(pool):
            pool.memset(ident, 0.0).then_inc(S["consts"], 1)
            pool.wait_ge(S["consts"], 1)
            pool.affine_select(out=ident, in_=ident, compare_op=ALU.not_equal, fill=1.0, base=0,
                               pattern=[[-1, D]], channel_multiplier=1).then_inc(S["consts"], 1)
            pool.iota(WT[:, 0, :], [[WC // 2, NWIN]], base=0, channel_multiplier=0,
                      allow_small_or_imprecise_dtypes=True).then_inc(S["consts"], 1)
            pool.memset(WT[:, 1, :], 0.0).then_inc(S["consts"], 1)
            pool.memset(ZZ, 0.0).then_inc(S["consts"], 1)
            pool.memset(ones, 1.0 / HALF).then_inc(S["consts"], 1)
            pool.iota(iotax, [[1, WC], [0, KH]], base=0, channel_multiplier=0,
                      allow_small_or_imprecise_dtypes=True).then_inc(S["consts"], 1)
            pool.memset(KL[:, :, EC:ECP], -1.0).then_inc(S["consts"], 1)
            pool.wait_ge(S["keys_turned"], 4)
            pool.memset(LR[:, :, P:P + 1, :], 1.0).then_inc(S["consts"], 1)
            pool.memset(LR[:, :, P + 1:128, :], 0.0).then_inc(S["consts"], 1)
            pool.wait_ge(S["dve_step"], step_at["bounds"])
            pool.iota(CF, [[-1, EC]], base=int(BIG), channel_multiplier=0,
                      allow_small_or_imprecise_dtypes=True).then_inc(S["consts"], 1)
            pool.iota(CI, [[1, EC]], base=1, channel_multiplier=0,
                      allow_small_or_imprecise_dtypes=True).then_inc(S["consts"], 1)
            pool.iota(WID, [[1, 2]], base=0, channel_multiplier=2,
                      allow_small_or_imprecise_dtypes=True).then_inc(S["consts"], 1)
            pool.wait_ge(S["sums_ready"], 1)
            pool.partition_all_reduce(sq, sq, 128, bass.bass_isa.ReduceOp.add).then_inc(S["sums_done"], 1)
            pool.wait_ge(S["max_ready"], 1)
            pool.partition_all_reduce(mx, mx, 128, bass.bass_isa.ReduceOp.max).then_inc(S["max_done"], 1)

            pool.wait_ge(S["tab_back"], 16)
            pool.wait_ge(S["keys_kept"], 4)
            pool.sem_inc(S["hot_ready"], 4 * RR)
            done = pool.alloc_register("pool_steps_done")
            chunk = pool.alloc_register("pool_chunk")
            pool.reg_mov(done, 0)
            regs = [pool.alloc_register(f"pool_{what}{q}") for q in range(WQ) for what in ("first", "count")]

            def rel_keys(c, w):
                t = pool.snap(done, min_val=0, max_val=1 << 20)
                slot = t & (RR - 1)
                pool.wait_ge(S["hot_ready"], t * 4 + 4)
                pool.tensor_tensor(KR[:, bass.ds(slot * (2 * K), 2 * K)].rearrange("p (t k) -> p t k", t=2),
                                   KL[:, :, bass.ds(c, K)], WT[:, :, bass.ds(w, 1)].broadcast_to([P, 2, K]),
                                   ALU.subtract).then_inc(S["key_rel"], 1)
                pool.reg_add(done, done, 1)

            with pool.Fori(0, NWIN // WQ) as quad:
                pool.load(regs, TAB[0:1, bass.ds(quad * (2 * WQ), 2 * WQ)])
                for q in range(WQ):
                    pool.reg_mov(chunk, regs[2 * q])
                    count = pool.snap(regs[2 * q + 1], min_val=1, max_val=EC // K)
                    with pool.Fori(0, count) as _i:
                        rel_keys(pool.snap(chunk, min_val=0, max_val=EC - 1), quad * WQ + q)
                        pool.reg_add(chunk, chunk, K)
            rel_keys(0, 0)
            pool.memset(CNTF[:, 1:2], 0.0).then_inc(S["keys_made"], 1)

        CONST_EARLY, CONST_IOTAX, CONST_ALL = 6, 7, 13

        @block.vector
        def _(dve):
            n = [0]
            made = {}

            def step(ins, name=None):
                if name is None:
                    n[0] += 1
                    ins.then_inc(S["dve_step"], 1)
                    dve.wait_ge(S["dve_step"], n[0])
                else:
                    made[name] = made.get(name, 0) + 1
                    ins.then_inc(S[name], 1)
                    dve.wait_ge(S[name], made[name])

            dve.wait_ge(S["edges_in"], 16)
            step(dve.tensor_copy(df, di))
            step(dve.tensor_scalar(dw, df, 1.0 / W, -0.5 + 0.5 / W, ALU.mult, ALU.add))
            step(dve.tensor_scalar(dw, dw, ROUND, None, ALU.add))
            step(dve.tensor_scalar(dw, dw, ROUND, None, ALU.subtract))
            dwv = dw.rearrange("p (j i) -> p j i", j=EJ)
            dve.tensor_reduce(CM[:, 0:EJ], dwv, AX.X, ALU.max)
            step(dve.tensor_reduce(CM[:, EJ:2 * EJ], dwv, AX.X, ALU.min))
            step(dve.scalar_tensor_tensor(df, dw, float(WC - W), df, ALU.mult, ALU.add))
            step(dve.tensor_copy(dw, df))
            assert n[0] == step_at["bounds"]
            dve.wait_ge(S["sources_in"], 16)
            step(dve.tensor_copy(ef, ei))
            step(dve.tensor_scalar(eh, ef, 1.0 / P, -0.5 + 0.5 / P, ALU.mult, ALU.add))
            step(dve.tensor_scalar(eh, eh, ROUND, None, ALU.add))
            step(dve.tensor_scalar(eh, eh, ROUND, None, ALU.subtract))
            step(dve.scalar_tensor_tensor(es, eh, -float(P), ef, ALU.mult, ALU.add))
            step(dve.scalar_tensor_tensor(dw, eh, float(W), dw, ALU.mult, ALU.add))
            assert n[0] == step_at["keyd"]
            dve.wait_ge(S["rows_mm"], 1)
            dve.tensor_tensor(row[:, 2 * D:3 * D], ps[7][0:1, 0:D], row[:, 0:D], ALU.add).then_inc(S["gate_pre"], 1)
            dve.tensor_tensor(gb[:, 0:2], gb[:, 0:2], gb[:, 3:5], ALU.add)
            dve.wait_ge(S["weights_in"], 16 * 18)
            for j, w in enumerate((WR[:, 0:D], WR[:, D:2 * D], W31R)):
                step(dve.tensor_tensor_reduce(SQT, w, w, 1.0, 0.0, ALU.mult, ALU.add, sq[:, j:j + 1]),
                     None if j < 2 else "sums_ready")
            dve.scalar_tensor_tensor(mx[:, 0:2], bc, -1.0, bc, ALU.mult, ALU.max)
            dve.memset(mx[:, 2:3], 0.0)
            dve.wait_ge(S["gate_done"], 1)
            step(dve.tensor_tensor(row[:, 3 * D:4 * D], row[:, 2 * D:3 * D], row[:, D:2 * D], ALU.mult))
            dve.tensor_tensor(row[:, 3 * D:4 * D], row[:, 3 * D:4 * D], ps[7][0:1, D:2 * D],
                              ALU.add).then_inc(S["rows_done"], 1)
            for g in range(4):
                dve.wait_ge(S["keys_turned"], g + 1)
                to = KL[:, g // 2, 0:EC].rearrange("p (c j) -> p j c", j=EJ)[:, 4 * (g % 2):4 * (g % 2) + 4, :]
                dve.tensor_scalar(to, ps[6][0:P, 0:4 * EP].rearrange("p (j c) -> p j c", j=4),
                                  HALF, None, ALU.mult).then_inc(S["keys_kept"], 1)
            dve.wait_ge(S["consts"], CONST_IOTAX)
            step(dve.tensor_scalar(iotax, iotax, HALF, None, ALU.mult))
            dve.wait_ge(S["cm_back"], 32)
            dve.wait_ge(S["consts"], CONST_ALL)
            for q in range(2):
                step(dve.scalar_tensor_tensor(TMP, CB[:, 0:EC], WID[:, q:q + 1], CF, ALU.is_ge, ALU.mult))
                step(dve.tensor_reduce(WM[:, q:q + 1], TMP, AX.X, ALU.max))
                step(dve.scalar_tensor_tensor(TMP, CB[:, EC:2 * EC], WID[:, q:q + 1], CI, ALU.is_le, ALU.mult))
                step(dve.tensor_reduce(WM[:, 2 + q:3 + q], TMP, AX.X, ALU.max))
            step(dve.tensor_scalar(WM[:, 0:2], WM[:, 0:2], -1.0, BIG, ALU.mult, ALU.add))
            step(dve.tensor_scalar(WM[:, 0:2], WM[:, 0:2], float(EC - 1), None, ALU.min))
            step(dve.tensor_tensor(WM[:, 4:6], WM[:, 2:4], WM[:, 0:2], ALU.subtract))
            step(dve.tensor_scalar(WM[:, 4:6], WM[:, 4:6], 1.0 / K, 0.5 - 0.5 / K, ALU.mult, ALU.add))
            tb = TBI.rearrange("p (q k) -> p q k", q=2)
            step(dve.tensor_scalar(WM[:, 4:6], WM[:, 4:6], ROUND, None, ALU.add))
            step(dve.tensor_scalar(WM[:, 4:6], WM[:, 4:6], ROUND, None, ALU.subtract))
            step(dve.tensor_scalar(WM[:, 4:6], WM[:, 4:6], 1.0, None, ALU.max))
            dve.tensor_copy(tb[:, :, 0:1], WM[:, 0:2].rearrange("p (q k) -> p q k", k=1))
            step(dve.tensor_copy(tb[:, :, 1:2], WM[:, 4:6].rearrange("p (q k) -> p q k", k=1)))
            assert n[0] == step_at["table"], n[0]

            dve.wait_ge(S["x_early"], 16)
            dve.tensor_reduce(mx[0:P, 2:3], XE, AX.X, ALU.max)
            step(dve.tensor_reduce(bd[0:P, 0:1], XE, AX.X, ALU.min))
            step(dve.scalar_tensor_tensor(mx[0:P, 2:3], bd[0:P, 0:1], -1.0, mx[0:P, 2:3], ALU.mult, ALU.max),
                 "max_ready")
            dve.wait_ge(S["tab_back"], 16)
            step(dve.tensor_copy(CNTF, TAB.rearrange("p (w k) -> p w k", k=2)[:, :, 1:2]))
            step(dve.tensor_reduce(TOTF, CNTF, AX.X, ALU.add))
            step(dve.tensor_scalar(TOTF, TOTF, 0.5, 0.25, ALU.mult, ALU.add))
            step(dve.tensor_scalar(TOTF, TOTF, ROUND, None, ALU.add))
            step(dve.tensor_scalar(TOTF, TOTF, ROUND, None, ALU.subtract))
            step(dve.tensor_copy(TOT, TOTF))
            pairs = dve.alloc_register("dve_pairs")
            dve.load(pairs, TOT)
            with dve.Fori(0, dve.snap(pairs, min_val=1, max_val=NWIN * EC // K)) as i:
                for r in range(RR):
                    dve.wait_ge(S["key_rel"], i * RR + (r + 1))
                    for h in range(2):
                        dve.wait_ge(S["hot_free"], i * (2 * RR) + (2 * r + h + 1))
                        rel = KR[:, r * 2 * K:(r + 1) * 2 * K].rearrange("p (t k) -> p t k", t=2)
                        dve.tensor_tensor(LR[:, h, 0:P, :], iotax[:, 0:P, :],
                                          rel[:, 1:2, h * KH:(h + 1) * KH].broadcast_to([P, P, KH]),
                                          ALU.is_equal).then_inc(S["hot_ready"], 1)
                        dve.tensor_tensor(MR[:, h], iotax, rel[:, 0:1, h * KH:(h + 1) * KH].broadcast_to([P, WC, KH]),
                                          ALU.is_equal).then_inc(S["hot_ready"], 1)

            dve.memset(CNTF[:, 0:1], 0.0).then_inc(S["hot_made"], 1)

            dve.wait_ge(S["max_done"], 1)
            dve.wait_ge(S["bounds_root"], 1)
            dve.tensor_copy(bd[:, 0:1], mx[:, 2:3])
            step(dve.tensor_tensor(bd[:, 1:2], sq[:, 0:1], sq[:, 1:2], ALU.add))
            step(dve.scalar_tensor_tensor(bd[:, 1:2], bd[:, 1:2], ROWB, mx[:, 0:1], ALU.mult, ALU.add))
            step(dve.scalar_tensor_tensor(bd[:, 2:3], sq[:, 2:3], ROWB, mx[:, 1:2], ALU.mult, ALU.add))
            step(dve.tensor_scalar(bd, bd, 2.0 ** -60, 2.0 ** 100, ALU.max, ALU.min))
            bi, sci, sii = bd.bitcast(I32), sc.bitcast(I32), si.bitcast(I32)
            step(dve.tensor_scalar(bi, bi, 23, None, ALU.logical_shift_right))
            step(dve.tensor_copy(sc, bi))
            dve.tensor_scalar(si, sc, -13.0, None, ALU.add)
            step(dve.tensor_scalar(sc, sc, -1.0, 268.0, ALU.mult, ALU.add))
            step(dve.tensor_copy(bi, sc))
            step(dve.tensor_scalar(sci, bi, 23, None, ALU.logical_shift_left))
            step(dve.tensor_copy(bi, si))
            step(dve.tensor_scalar(sii, bi, 23, None, ALU.logical_shift_left), "scales_ready")
            dve.wait_ge(S["keys_made"], 1)
            dve.wait_ge(S["deg_mm"], 1)
            deg = ps[7][0:P, 0:NC]
            dve.tensor_scalar(sd, deg, 1.0, None, ALU.add).then_inc(S["deg_plus"], 1)
            step(dve.tensor_scalar(s1, deg, 1.0, None, ALU.max))
            dve.reciprocal(s1, s1)
            dve.wait_ge(S["deg_root"], 1)
            step(dve.reciprocal(dinv, sd))

            def wait(name, v):
                if v:
                    dve.wait_ge(S[name], v)

            def evac(s, b):
                kind = STAGES[s][0]
                if kind not in ("gcn0", "gcn1", "gcn2"):
                    return
                o_, m = cols(b)
                wait("agg_done", val("agg_done", s, b))
                wait("dense_done", before("dense_done", s, b))
                wait("xt_ready", val("xt_ready", s - 1, b))
                agg = ps[val("agg_done", s, b) % 2][:, 0:m]
                scale = {"gcn0": si[:, 0:1], "gcn1": 1.0 / (SCALE * HALF), "gcn2": si[:, 2:3]}[kind]
                made["ag_ready"] = made.get("ag_ready", 0) + 1
                dve.scalar_tensor_tensor(AG[:, 0:m], agg, scale, XT[:, o_:o_ + m], ALU.mult,
                                         ALU.add).then_inc(S["ag_ready"], 1)

            def each(m, fn, name=None):
                for j in range(m):
                    ins = fn(j)
                step(ins, name)

            def norm(s, b, v, m, name=None):
                each(m, lambda j: dve.bn_stats(st[:, j, :], v[:, j, :]))
                each(m, lambda j: dve.bn_aggr(mv[:, j, :], st[:, j, :]))
                step(dve.tensor_scalar(rs[:, 0:m], mv[:, 0:m, 1], EPS, None, ALU.add), "var_ready")
                wait("sd_ready", val("sd_ready", s, b))
                step(dve.reciprocal(rs[:, 0:m], rs[:, 0:m]))
                each(m, lambda j: dve.tensor_scalar(v[:, j, :], v[:, j, :], mv[:, j, 0:1], rs[:, j:j + 1],
                                                    ALU.subtract, ALU.mult), name)

            def split2(v, cs, out, scale=SCALE):
                step(dve.tensor_scalar(out[0][:, cs, :], v, scale, None, ALU.mult))
                step(dve.scalar_tensor_tensor(out[1][:, cs, :], v, scale, out[0][:, cs, :], ALU.mult,
                                              ALU.subtract), "parts_done")

            def elem(s, b):
                kind, pin, pout = STAGES[s]
                m = chunks_of(b)
                c0 = START[b]
                cs = slice(c0, c0 + m)
                u, t = U2[b % 2][:, 0:m, :], T[:, 0:m, :]
                d0 = ps[2][0:P, 0:m * D].rearrange("p (c f) -> p c f", f=D)
                d1 = ps[3][0:P, 0:m * D].rearrange("p (c f) -> p c f", f=D)
                bb = BB.rearrange("p (a f) -> p a f", a=1).broadcast_to([P, m, D])

                def own(v, j):
                    return v[:, c0 + j:c0 + j + 1]

                if not kind.startswith("gru"):
                    if b >= 2:
                        wait("tf_done", plan.get(("tf_done", s, b - 2)))
                        for i in (f"x2_stored{b % 2}", f"out_stored{b % 2}"):
                            wait(i, plan.get((i, s, b - 2)))
                    else:
                        wait("tf_done", before("tf_done", s, 0))
                if kind == "prep":
                    wait("x_in", 16)
                    each(m, lambda j: dve.tensor_scalar(u[:, j, :], XALL[:, c0 + j, :], own(dinv, j), None, ALU.mult),
                         "u_ready")
                    split2(u, cs, pout, sc[0:P, 0:1])
                    return
                wait("stage_w", val("stage_w", s))
                if not kind.startswith("gru"):
                    wait("dense_done", val("dense_done", s, b))
                if kind in ("gcn0", "gcn1"):
                    each(m, lambda j: dve.scalar_tensor_tensor(u[:, j, :], d0[:, j, :], own(dinv, j), BB,
                                                               ALU.mult, ALU.add), "dense_free")
                if kind == "gcn0":
                    step(dve.tensor_scalar(t, u, 0.0, ab[:, 0:1], ALU.min, ALU.mult))
                    step(dve.scalar_tensor_tensor(u, u, 0.0, t, ALU.max, ALU.add))
                    wait("rx_in", val("rx_in", s, b))
                    step(dve.tensor_tensor(u, u, RX[:, 0:m, :], ALU.add), "rx_free")
                    norm(s, b, u, m, "u_ready")
                    split2(u, cs, pout)
                if kind in ("sage1", "sage2"):
                    step(dve.tensor_tensor(u, d1, bb, ALU.add))
                    each(m, lambda j: dve.scalar_tensor_tensor(u[:, j, :], d0[:, j, :], own(s1, j), u[:, j, :],
                                                               ALU.mult, ALU.add), "dense_free")
                if kind == "sage1":
                    step(dve.tensor_scalar(u, u, 0.0, None, ALU.max), "u_ready")
                    split2(u, cs, pout, sc[0:P, 1:2])
                if kind == "sage2":
                    step(dve.tensor_tensor(t, PB[0][:, cs, :], PB[1][:, cs, :], ALU.add))
                    step(dve.scalar_tensor_tensor(u, t, 1.0 / SCALE, u, ALU.mult, ALU.add))
                    norm(s, b, u, m, "u_ready")
                    split2(u, cs, pout)
                if kind == "gcn1":
                    step(dve.scalar_tensor_tensor(u, u, 0.2, u, ALU.mult, ALU.max))
                    each(m, lambda j: dve.tensor_scalar(u[:, j, :], u[:, j, :], own(dinv, j), None, ALU.mult),
                         "u_ready")
                    split2(u, cs, pout, sc[0:P, 2:3])
                if kind == "gcn2":
                    each(m, lambda j: dve.scalar_tensor_tensor(u[:, j, :], d0[:, j, :], own(dinv, j), WB[0:P],
                                                               ALU.mult, ALU.mult), "dense_free")
                    step(dve.tensor_tensor(u, u, bb, ALU.add))
                    step(dve.tensor_tensor(t, PB[0][:, cs, :], PB[1][:, cs, :], ALU.add))
                    step(dve.tensor_scalar(t, t, 1.0 / SCALE, None, ALU.mult))
                    each(m, lambda j: dve.scalar_tensor_tensor(u[:, j, :], t[:, j, :], own(sd, j), u[:, j, :],
                                                               ALU.mult, ALU.add))
                    norm(s, b, u, m, "u_ready")
                if kind.startswith("gru"):
                    o_, q = cols(b)
                    r, z, nx = GR[:, 0:q], GZ[:, 0:q], NX[:, 0:q]
                    wait("r_ready", val("r_ready", s, b))
                    step(dve.scalar_tensor_tensor(r, ps[5][:, 0:q], gb[:, 5:6], r, ALU.add, ALU.mult))
                    wait("z_ready", val("z_ready", s, b))
                    step(dve.tensor_tensor(r, r, ps[4][:, 0:q], ALU.add), "pre_n")
                    wait("n_ready", val("n_ready", s, b))
                    wait("tn_done", before("tn_done", s, b))
                    wait("nx_copied", before("nx_copied", s, b))
                    step(dve.tensor_tensor(nx, XT[:, o_:o_ + q], r, ALU.subtract))
                    step(dve.tensor_tensor(nx, nx, z, ALU.mult))
                    step(dve.tensor_tensor(nx, nx, r, ALU.add), "nx_ready")
                    wait("tn_done", val("tn_done", s, b))
                    tn = ps[6][0:P, 0:m * D].rearrange("p (c f) -> p c f", f=D)
                    if kind == "gru":
                        split2(tn, cs, pout)
                    else:
                        wait("rx_in", val("rx_in", s, b))
                        wait("tf_done", before("tf_done", s, b))
                        y = X3[:, 0:m, :]
                        step(dve.scalar_tensor_tensor(y, X2[:, 0:m, :], 2.0, tn, ALU.mult, ALU.add), "tn_free")
                        norm(s, b, y, m)
                        each(m, lambda j: dve.tensor_scalar(y[:, j, :], y[:, j, :], own(dinv, j), None, ALU.mult),
                         "u_ready")
                        split2(y, cs, pout)

            for s in range(NS):
                if STAGES[s][0] == "prep":
                    for b in range(NB):
                        elem(s, b)
                    continue
                evac(s, 0)
                for b in range(NB):
                    if b + 1 < NB:
                        evac(s, b + 1)
                    elem(s, b)

        @block.tensor
        def _(pe):
            pe.wait_ge(S["weights_in"], 16 * 18)
            pe.wait_ge(S["consts"], CONST_EARLY)
            for g in range(4):
                for k in range(4 * g, min(4 * g + 4, 14)):
                    i = pe.transpose(ps[g][:, (k % 4) * D:(k % 4 + 1) * D], WR[:, k * D:(k + 1) * D], ident)
                i.then_inc(S["weights_turned"], 1)
            pe.matmul(ps[7][0:1, 0:D], ctxc, WGB[:, 0:D], start=True, stop=True)
            pe.matmul(ps[7][0:1, D:2 * D], ctxc, WGB[:, D:2 * D], start=True, stop=True).then_inc(S["rows_mm"], 1)
            pe.wait_ge(S["turned_kept"], 4)
            for l in range(4):
                pe.matmul(ps[l][:, 0:3 * D], TW[:, (10 + l) * D:(11 + l) * D], TW[:, 4 * D:7 * D],
                          start=True, stop=True).then_inc(S["wc_mm"], 1)
            for g in range(4):
                if g == 0:
                    pe.wait_ge(S["dve_step"], step_at["keyd"])
                else:
                    pe.wait_ge(S["keys_kept"], g)
                what = dw if g < 2 else es
                for j in range(4):
                    jj = 4 * (g % 2) + j
                    i = pe.transpose(ps[6][0:P, j * EP:(j + 1) * EP], what[:, jj * P:(jj + 1) * P], ident[0:EP, 0:EP])
                i.then_inc(S["keys_turned"], 1)

            pe.wait_ge(S["tab_back"], 16)
            pe.wait_ge(S["wc_done"], 4)
            done = pe.alloc_register("pe_steps_done")
            pe.reg_mov(done, 0)
            pe.sem_inc(S["hot_free"], 2)
            regs = [pe.alloc_register(f"pe_{what}{q}") for q in range(WQ) for what in ("first", "count")]

            def window(w, q, bank):
                count = pe.snap(regs[2 * q + 1], min_val=1, max_val=EC // K)
                pe.wait_ge(S["win_kept"], w + 1)
                pe.matmul(ps[bank][:, 0:2], ZZ, ZZ[:, 0:2], start=True, stop=False, skip_group_check=True)
                with pe.Fori(0, count) as _i:
                    t = pe.snap(done, min_val=0, max_val=1 << 20)
                    for h in range(2):
                        pe.wait_ge(S["hot_ready"], t * 4 + (4 * RR + 2 * h + 2))
                        for k in range(KH):
                            i = pe.matmul(ps[bank][:, 0:WC], LR[:, h, :, k], MR[:, h, :, k], start=False, stop=False,
                                          skip_group_check=True)
                        i.then_inc(S["hot_free"], 1)
                    pe.reg_add(done, done, 1)
                pe.matmul(ps[bank][:, 0:2], ZZ, ZZ[:, 0:2], start=False, stop=True,
                          skip_group_check=True).then_inc(S["win_done"], 1)

            with pe.Fori(0, NWIN // WQ) as quad:
                pe.load(regs, TAB[0:1, bass.ds(quad * (2 * WQ), 2 * WQ)])
                for q in range(WQ):
                    window(quad * WQ + q, q, q % 2)

            pe.wait_ge(S["deg_in"], 16)
            for c in range(NC):
                i = pe.matmul(ps[7][0:P, c:c + 1], DEGR[:, c * P:(c + 1) * P], ones[0:NC, 0:1], start=True, stop=True)
            i.then_inc(S["deg_mm"], 1)

            def wait(name, v):
                if v:
                    pe.wait_ge(S[name], v)

            def spmm(s, b, first=0, last=NC):
                pin = STAGES[s][1]
                o_, m = cols(b)
                g = val("agg_done", s, b)
                if g > 2 and first == 0:
                    wait("ag_ready", g - 2)
                agg = ps[g % 2][:, 0:m]
                for k in range(first, last):
                    if b == 0 and k in START:
                        c = START.index(k)
                        if s == 1:
                            turn_rows(0, c)
                        wait("parts_done", val("parts_done", s - 1, c))
                    for q, part in enumerate(pin):
                        i = pe.matmul(agg, part[:, k, :], AT[:, k, o_:o_ + m], start=k == 0 and q == 0,
                                      stop=k == NC - 1 and q == len(pin) - 1)
                if last == NC:
                    i.then_inc(S["agg_done"], 1)

            def dense(s, b):
                kind = STAGES[s][0]
                o_, m = cols(b)
                if b == 0:
                    wait("stage_w", val("stage_w", s))
                wait("ag_ready", val("ag_ready", s, b))
                wait("dense_free", before("dense_free", s, b))
                wait("pre_n", before("pre_n", s, b))
                if kind.startswith("gru"):
                    xt = XT[:, o_:o_ + m]
                    if STAGES[s - 1][0] == "gru":
                        wait("nx_copied", val("nx_copied", s - 1, b))
                    else:
                        wait("xt_ready", val("xt_ready", s - 1, b))
                    for g in range(2):
                        pe.matmul(ps[2 + g][:, 0:m], WCG[:, g * D:(g + 1) * D], AG[:, 0:m], start=True, stop=False)
                        pe.matmul(ps[2 + g][:, 0:m], WHH[:, g * D:(g + 1) * D], xt, start=False, stop=True)
                    pe.matmul(ps[4][:, 0:m], WCG[:, 2 * D:3 * D], AG[:, 0:m], start=True, stop=True)
                    i = pe.matmul(ps[5][:, 0:m], WHH[:, 2 * D:3 * D], xt, start=True, stop=True)
                else:
                    if kind.startswith("sage"):
                        wait("xs_ready", val("xs_ready", s, b))
                    for j in range(chunks_of(b)):
                        i = pe.matmul(ps[2][0:P, j * D:(j + 1) * D], AG[:, j * P:(j + 1) * P], WA,
                                      start=True, stop=True)
                        if kind.startswith("sage"):
                            i = pe.matmul(ps[3][0:P, j * D:(j + 1) * D], XS[:, j * P:(j + 1) * P], WB,
                                          start=True, stop=True)
                i.then_inc(S["dense_done"], 1)

            def turn_new(s, b):
                if STAGES[s][0].startswith("gru"):
                    wait("nx_ready", val("nx_ready", s, b))
                    prev = (s, b - 1) if b else (s - 1, NB - 1)
                    if STAGES[prev[0]][0] == "gru":
                        wait("parts_done", val("parts_done", *prev))
                    elif b:
                        wait("tn_free", val("tn_free", *prev))
                    for j in range(chunks_of(b)):
                        i = pe.transpose(ps[6][0:P, j * D:(j + 1) * D], NX[:, j * P:(j + 1) * P], ident)
                    i.then_inc(S["tn_done"], 1)

            def turn_rows(s, b):
                if ("tf_done", s, b) in plan:
                    wait("u_ready", val("u_ready", s, b))
                    wait("xt_ready", before("xt_ready", s, b))
                    v = X3 if STAGES[s][0] == "gru_last" else U2[b % 2]
                    for j in range(chunks_of(b)):
                        i = pe.transpose(ps[7][:, j * P:(j + 1) * P], v[:, j, :], ident[0:P, 0:P])
                    i.then_inc(S["tf_done"], 1)

            sooner, early, late = START[NB - 4], START[NB - 2], START[NB - 1]
            for s in range(1, NS):
                last_gru = STAGES[s - 1][0] == "gru_last"
                spmm(s, 0, 0 if s == 1 else sooner, early)
                turn_new(s - 1, NB - 2)
                if s > 1 and not last_gru:
                    turn_rows(s - 1, NB - 2)
                spmm(s, 1, 0, early)
                turn_new(s - 1, NB - 1)
                if s > 1:
                    turn_rows(s - 1, NB - 2 if last_gru else NB - 1)
                spmm(s, 0, early, late)
                spmm(s, 1, early, late)
                spmm(s, 0, late)
                spmm(s, 1, late)
                if last_gru:
                    turn_rows(s - 1, NB - 1)
                for b in range(NB):
                    if 0 < b < NB - 1:
                        spmm(s, b + 1)
                    if b == NB - 1 and s + 1 < NS:
                        spmm(s + 1, 0, 0, sooner)
                    dense(s, b)
                    lag = 2 if STAGES[s][0] == "gru_last" else 1
                    if lag <= b and b - lag < NB - 2:
                        turn_rows(s, b - lag)
                    if 0 < b < NB - 1:
                        turn_new(s, b - 1)

        @block.scalar
        def _(act):
            for g in range(4):
                act.wait_ge(S["weights_turned"], g + 1)
                m = (4 if g < 3 else 2) * D
                act.activation(TW[:, 4 * g * D:4 * g * D + m], ps[g][:, 0:m], ACT.Copy).then_inc(S["turned_kept"], 1)
            for l in range(4):
                act.wait_ge(S["wc_mm"], l + 1)
                act.activation(WCT[:, 3 * D * l:3 * D * (l + 1)], ps[l][:, 0:3 * D], ACT.Copy).then_inc(S["wc_done"], 1)
            act.wait_ge(S["gate_pre"], 1)
            act.activation(row[:, 2 * D:3 * D], row[:, 2 * D:3 * D], ACT.Sigmoid).then_inc(S["gate_done"], 1)

            act.wait_ge(S["wc_kept"], 48)
            act.sem_inc(S["win_kept"], 2)

            def keep(w, bank, m):
                act.wait_ge(S["win_done"], w + 1)
                v = ps[bank][0:P + 1, 0:WC].rearrange("p (c d) -> p c d", d=W)[:, :, 0:m]
                act.activation(ATX[:, :, bass.ds(w * W, m)], v, ACT.Copy, scale=HALF).then_inc(S["win_kept"], 1)

            with act.Fori(0, NWIN // 2 - 1) as pair:
                keep(pair * 2, 0, W)
                keep(pair * 2 + 1, 1, W)
            keep(NWIN - 2, 0, W)
            keep(NWIN - 1, 1, LASTW)

            act.wait_ge(S["sums_done"], 1)
            act.activation(sq, sq, ACT.Sqrt).then_inc(S["bounds_root"], 1)
            act.wait_ge(S["deg_plus"], 1)
            act.activation(sd, sd, ACT.Sqrt).then_inc(S["deg_root"], 1)

            def wait(name, v):
                if v:
                    act.wait_ge(S[name], v)

            def evac(s, b):
                kind = STAGES[s][0]
                if kind not in ("sage1", "sage2", "gru", "gru_last"):
                    return
                o_, m = cols(b)
                wait("dense_done", before("dense_done", s, b))
                if kind.startswith("sage"):
                    if b == 0:
                        wait("rx_free", total["rx_free"])
                    wait("xt_ready", val("xt_ready", s - 1, b))
                    act.activation(XS[:, 0:m], XT[:, o_:o_ + m], ACT.Copy).then_inc(S["xs_ready"], 1)
                wait("agg_done", val("agg_done", s, b))
                agg = ps[val("agg_done", s, b) % 2][:, 0:m]
                scale = si[:, 1:2] if kind == "sage2" else 1.0 / (SCALE * HALF)
                wait("scales_ready", 1)
                act.activation(AG[:, 0:m], agg, ACT.Copy, scale=scale).then_inc(S["ag_ready"], 1)

            def keep_turned(s, b):
                if ("xt_ready", s, b) in plan:
                    o_, m = cols(b)
                    wait("tf_done", val("tf_done", s, b))
                    act.activation(XT[:, o_:o_ + m], ps[7][:, 0:m], ACT.Copy).then_inc(S["xt_ready"], 1)

            def gates(s, b):
                kind = STAGES[s][0]
                o_, q = cols(b)
                m = chunks_of(b)
                if kind.startswith("gru"):
                    wait("dense_done", val("dense_done", s, b))
                    wait("x2_stored0", total["x2_stored0"])
                    wait("x2_stored1", total["x2_stored1"])
                    wait("tf_done", before("tf_done", 4, 0))
                    wait("parts_done", before("parts_done", 4, 0))
                    wait("nx_ready", before("nx_ready", s, b))
                    act.activation(GR[:, 0:q], ps[2][:, 0:q], ACT.Sigmoid, bias=gb[:, 0:1]).then_inc(S["r_ready"], 1)
                    act.activation(GZ[:, 0:q], ps[3][:, 0:q], ACT.Sigmoid, bias=gb[:, 1:2]).then_inc(S["z_ready"], 1)
                    wait("pre_n", val("pre_n", s, b))
                    act.activation(GR[:, 0:q], GR[:, 0:q], ACT.Tanh, bias=gb[:, 2:3]).then_inc(S["n_ready"], 1)
                if kind == "gru":
                    wait("nx_ready", val("nx_ready", s, b))
                    act.activation(XT[:, o_:o_ + q], NX[:, 0:q], ACT.Copy).then_inc(S["nx_copied"], 1)
                if kind in ("gcn0", "sage2", "gru_last", "gcn2"):
                    wait("var_ready", val("var_ready", s, b))
                    act.activation(rs[:, 0:m], rs[:, 0:m], ACT.Sqrt).then_inc(S["sd_ready"], 1)

            for b in range(NB):
                keep_turned(0, b)
            for s in range(1, NS):
                evac(s, 0)
                for b in range(NB):
                    if b + 1 < NB:
                        evac(s, b + 1)
                    lag = 2 if STAGES[s][0] == "gru_last" else 1
                    if lag <= b and b - lag < NB - 2:
                        keep_turned(s, b - lag)
                    gates(s, b)
                keep_turned(s, NB - 2)
                keep_turned(s, NB - 1)


_INS = ['x', 'src', 'dst', 'L0_gnn_W', 'L0_gnn_b', 'L0_gnn_a', 'L1_gnn_W1_l', 'L1_gnn_b1', 'L1_gnn_W1_r',
        'L1_gnn_W2_l', 'L1_gnn_b2', 'L1_gnn_W2_r', 'L2_gnn_weight', 'L2_gnn_w_ih', 'L2_gnn_w_hh', 'L2_gnn_b_ih',
        'L2_gnn_b_hh', 'L3_gnn_ctx', 'L3_gnn_W1', 'L3_gnn_b1', 'L3_gnn_W2', 'L3_gnn_b2', 'L3_gnn_Wg', 'L3_gnn_bg',
        'L3_gnn_Wb']

_OUT = ((N, D), "float32")


def kernel(**inputs):
    import numpy as np
    import concourse.bacc as bacc
    from concourse.bass_utils import run_bass_kernel_spmd

    nc = bacc.Bacc("TRN2", target_bir_lowering=False, num_devices=1)
    arrays, args = {}, []
    for name in _INS:
        a = np.ascontiguousarray(inputs[name])
        if a.ndim == 0:
            a = a.reshape(1)
        arrays[f"in_{name}"] = a
        args.append(nc.dram_tensor(f"in_{name}", a.shape, mybir.dt.from_np(a.dtype), kind="ExternalInput").ap())
    out = nc.dram_tensor("out", _OUT[0], mybir.dt.from_np(np.dtype(_OUT[1])), kind="ExternalOutput").ap()
    build(nc, *args, out)
    r = run_bass_kernel_spmd(nc, [arrays], core_ids=[0])
    return r.results[0]["out"]
```
